# Optimizing a Trainium2 kernel written in Bass

```python
import numpy as np
import jax
import jax.numpy as jnp

def _softmax(x, axis=-1):
    return jax.nn.softmax(x, axis=axis)

def _gelu(x):
    return jax.nn.gelu(x, approximate=True)

def _silu(x):
    return jax.nn.silu(x)

def _sigmoid(x):
    return jax.nn.sigmoid(x)

def _layernorm(x, axis=-1, eps=1e-05):
    m = jnp.mean(x, axis=axis, keepdims=True)
    v = jnp.var(x, axis=axis, keepdims=True)
    return (x - m) / jnp.sqrt(v + eps)

def _scatter_add(tgt, idx, src, axis=0):
    return tgt.at[idx].add(src)

def _segment_sum(src, seg, n):
    return jax.ops.segment_sum(src, seg, n)
kernel_name = 'mk_cond_resid_d4_seqx_r2_62f061'

def setup_inputs(seed: int=0):
    np.random.seed(seed)
    _w = jnp.asarray

    def _rec_inputs():
        import jax
        import jax.numpy as jnp
        _rk = jax.random.key(seed)
        x = -0.000125 + 0.9999 * jax.random.normal(jax.random.fold_in(_rk, 1), (2, 2048, 512), jnp.float32)
        _lenS = 2048 - jax.random.randint(jax.random.fold_in(_rk, 7), (2,), 0, max(1, 2048 // 4) + 1, jnp.int32)
        _lenS2 = 2048 - jax.random.randint(jax.random.fold_in(_rk, 8), (2,), 0, max(1, 2048 // 4) + 1, jnp.int32)
        cond_1024 = -0.00493535 + 1.00056 * jax.random.normal(jax.random.fold_in(_rk, 11), (2, 512), jnp.float32)
        return (x, cond_1024)
    x, cond_1024 = _rec_inputs()

    def _L0_cond_setup():
        import jax, jax.numpy as jnp
        import numpy as np
        N, T, D, H = (64, 256, 512, 512)
        key = jax.random.key(seed)
        k1, k2, k3, k4 = jax.random.split(key, 4)
        x = jax.random.normal(k1, (N, T, D), dtype=jnp.float32)
        h0 = jax.random.normal(k2, (N, H), dtype=jnp.float32)
        Wx = jax.random.normal(k3, (D, H), dtype=jnp.float32) / np.sqrt(D)
        Wh = jax.random.normal(k4, (H, H), dtype=jnp.float32) / np.sqrt(H)
        b = jnp.zeros((H,), dtype=jnp.float32)
        return {'x': x, 'h0': h0, 'Wx': Wx, 'Wh': Wh, 'b': b}
    _L0_cond_all = _L0_cond_setup()
    _L0_cond_in = {k: v for k, v in _L0_cond_all.items() if k in ('Wx', 'Wh', 'b')}
    del _L0_cond_all

    def _L1_cond_setup():
        import jax, jax.numpy as jnp
        import numpy as np
        key = jax.random.key(seed)
        k1, k2 = jax.random.split(key)
        B, S, D = (32, 1024, 512)
        query = jax.random.normal(k1, (B, D), dtype=jnp.float32)
        values = jax.random.normal(k2, (B, S, D), dtype=jnp.float32)
        return {'query': query, 'values': values}
    _L1_cond_all = _L1_cond_setup()
    _L1_cond_in = {k: v for k, v in _L1_cond_all.items() if k in ()}
    del _L1_cond_all

    def _L2_cond_setup():
        import jax, jax.numpy as jnp
        import numpy as np
        B, S, I, H = (16, 1024, 512, 512)
        key = jax.random.key(seed)
        ks = jax.random.split(key, 6)
        scale_ih = 1.0 / np.sqrt(I)
        scale_hh = 1.0 / np.sqrt(H)
        return {'x': jax.random.normal(ks[0], (B, S, I), dtype=jnp.float32), 'hx': jax.random.normal(ks[1], (B, H), dtype=jnp.float32), 'W_ih': jax.random.normal(ks[2], (H, I), dtype=jnp.float32) * scale_ih, 'W_hh': jax.random.normal(ks[3], (H, H), dtype=jnp.float32) * scale_hh, 'b_ih': jax.random.normal(ks[4], (H,), dtype=jnp.float32) * scale_ih, 'b_hh': jax.random.normal(ks[5], (H,), dtype=jnp.float32) * scale_hh}
    _L2_cond_all = _L2_cond_setup()
    _L2_cond_in = {k: v for k, v in _L2_cond_all.items() if k in ('W_ih', 'W_hh', 'b_ih', 'b_hh')}
    del _L2_cond_all

    def _L3_cond_setup():
        import jax, jax.numpy as jnp
        import numpy as np
        INPUT_DIM = 512
        HIDDEN_DIM = 512
        CHUNK_SIZE = 4

        def _linear_params(key, fan_in, fan_out):
            kw, kb = jax.random.split(key)
            bound = 1.0 / np.sqrt(fan_in)
            W = jax.random.uniform(kw, (fan_in, fan_out), jnp.float32, -bound, bound)
            b = jax.random.uniform(kb, (fan_out,), jnp.float32, -bound, bound)
            return (W, b)

        def _gru_forward(x, h0, Wz, bz, Wr, br, Wh, bh, Wp, bp):
            B, T, D = x.shape
            t = jnp.arange(T)
            do_prop = ((t + 1) % CHUNK_SIZE == 0) & (t < T - 1)
            xs = jnp.transpose(x, (1, 0, 2))

            def step(h, inp):
                x_t, prop = inp
                comb = jnp.concatenate([x_t, h], axis=-1)
                z = jax.nn.sigmoid(comb @ Wz + bz)
                r = jax.nn.sigmoid(comb @ Wr + br)
                comb2 = jnp.concatenate([x_t, r * h], axis=-1)
                h_cand = jnp.tanh(comb2 @ Wh + bh)
                h_new = (1.0 - z) * h + z * h_cand
                h_next = jnp.where(prop, jnp.tanh(h_new @ Wp + bp), h_new)
                return (h_next, h_new)
            _, ys = jax.lax.scan(step, h0, (xs, do_prop))
            return jnp.transpose(ys, (1, 0, 2))
        key = jax.random.key(seed)
        ks = jax.random.split(key, 6)
        x = jax.random.normal(ks[0], (64, 256, INPUT_DIM), jnp.float32)
        h0 = jax.random.normal(ks[1], (64, HIDDEN_DIM), jnp.float32)
        Wz, bz = _linear_params(ks[2], INPUT_DIM + HIDDEN_DIM, HIDDEN_DIM)
        Wr, br = _linear_params(ks[3], INPUT_DIM + HIDDEN_DIM, HIDDEN_DIM)
        Wh, bh = _linear_params(ks[4], INPUT_DIM + HIDDEN_DIM, HIDDEN_DIM)
        Wp, bp = _linear_params(ks[5], HIDDEN_DIM, HIDDEN_DIM)
        return {'x': x, 'h0': h0, 'Wz': Wz, 'bz': bz, 'Wr': Wr, 'br': br, 'Wh': Wh, 'bh': bh, 'Wp': Wp, 'bp': bp}
    _L3_cond_all = _L3_cond_setup()
    _L3_cond_in = {k: v for k, v in _L3_cond_all.items() if k in ('Wz', 'bz', 'Wr', 'br', 'Wh', 'bh', 'Wp', 'bp')}
    del _L3_cond_all
    return {'x': x, 'cond_1024': cond_1024, 'L0_cond_Wx': _L0_cond_in['Wx'], 'L0_cond_Wh': _L0_cond_in['Wh'], 'L0_cond_b': _L0_cond_in['b'], 'L2_cond_W_ih': _L2_cond_in['W_ih'], 'L2_cond_W_hh': _L2_cond_in['W_hh'], 'L2_cond_b_ih': _L2_cond_in['b_ih'], 'L2_cond_b_hh': _L2_cond_in['b_hh'], 'L3_cond_Wz': _L3_cond_in['Wz'], 'L3_cond_bz': _L3_cond_in['bz'], 'L3_cond_Wr': _L3_cond_in['Wr'], 'L3_cond_br': _L3_cond_in['br'], 'L3_cond_Wh': _L3_cond_in['Wh'], 'L3_cond_bh': _L3_cond_in['bh'], 'L3_cond_Wp': _L3_cond_in['Wp'], 'L3_cond_bp': _L3_cond_in['bp']}

def reference(x, cond_1024, L0_cond_Wx, L0_cond_Wh, L0_cond_b, L2_cond_W_ih, L2_cond_W_hh, L2_cond_b_ih, L2_cond_b_hh, L3_cond_Wz, L3_cond_bz, L3_cond_Wr, L3_cond_br, L3_cond_Wh, L3_cond_bh, L3_cond_Wp, L3_cond_bp):
    import jax
    import jax.numpy as jnp

    def _L0_cond_ref(x, h0, Wx, Wh, b):
        import jax, jax.numpy as jnp
        import numpy as np
        N, T, D, H = (64, 256, 512, 512)
        xw = jnp.einsum('ntd,dh->nth', x, Wx) + b

        def step(prev_h, xw_t):
            next_h = jnp.tanh(prev_h @ Wh + xw_t)
            return (next_h, next_h)
        _, hs = jax.lax.scan(step, h0, jnp.swapaxes(xw, 0, 1))
        return jnp.swapaxes(hs, 0, 1)

    def _L1_cond_ref(query, values):
        import jax, jax.numpy as jnp
        import numpy as np
        D = query.shape[-1]
        weights = jnp.einsum('bd,bsd->bs', query, values) / jnp.sqrt(jnp.asarray(D, query.dtype))
        weights = jax.nn.softmax(weights, axis=0)
        return values * weights[..., None]

    def _L2_cond_ref(x, hx, W_ih, W_hh, b_ih, b_hh):
        import jax, jax.numpy as jnp
        import numpy as np
        B, S, I, H = (16, 1024, 512, 512)
        h_term = hx @ W_hh.T + b_hh + b_ih
        x_term = jnp.einsum('bsi,hi->bsh', x, W_ih)
        out = jnp.tanh(x_term + h_term[:, None, :])
        return out

    def _L3_cond_ref(x, h0, Wz, bz, Wr, br, Wh, bh, Wp, bp):
        import jax, jax.numpy as jnp
        import numpy as np
        INPUT_DIM = 512
        HIDDEN_DIM = 512
        CHUNK_SIZE = 4

        def _linear_params(key, fan_in, fan_out):
            kw, kb = jax.random.split(key)
            bound = 1.0 / np.sqrt(fan_in)
            W = jax.random.uniform(kw, (fan_in, fan_out), jnp.float32, -bound, bound)
            b = jax.random.uniform(kb, (fan_out,), jnp.float32, -bound, bound)
            return (W, b)

        def _gru_forward(x, h0, Wz, bz, Wr, br, Wh, bh, Wp, bp):
            B, T, D = x.shape
            t = jnp.arange(T)
            do_prop = ((t + 1) % CHUNK_SIZE == 0) & (t < T - 1)
            xs = jnp.transpose(x, (1, 0, 2))

            def step(h, inp):
                x_t, prop = inp
                comb = jnp.concatenate([x_t, h], axis=-1)
                z = jax.nn.sigmoid(comb @ Wz + bz)
                r = jax.nn.sigmoid(comb @ Wr + br)
                comb2 = jnp.concatenate([x_t, r * h], axis=-1)
                h_cand = jnp.tanh(comb2 @ Wh + bh)
                h_new = (1.0 - z) * h + z * h_cand
                h_next = jnp.where(prop, jnp.tanh(h_new @ Wp + bp), h_new)
                return (h_next, h_new)
            _, ys = jax.lax.scan(step, h0, (xs, do_prop))
            return jnp.transpose(ys, (1, 0, 2))
        return _gru_forward(x, h0, Wz, bz, Wr, br, Wh, bh, Wp, bp)
    x = x + _L0_cond_ref(x, cond_1024, L0_cond_Wx, L0_cond_Wh, L0_cond_b)
    x = x + _L1_cond_ref(cond_1024, x)
    x = x + _L2_cond_ref(x, cond_1024, L2_cond_W_ih, L2_cond_W_hh, L2_cond_b_ih, L2_cond_b_hh)
    x = x + _L3_cond_ref(x, cond_1024, L3_cond_Wz, L3_cond_bz, L3_cond_Wr, L3_cond_br, L3_cond_Wh, L3_cond_bh, L3_cond_Wp, L3_cond_bp)
    return x

_drawn_inputs = setup_inputs


def setup_inputs(seed=0):
    import zlib

    import numpy as np

    out = dict(_drawn_inputs(seed))
    spreads = {'L0_cond_b': (0.0, 0.1)}
    factors = {'L2_cond_b_ih': 5.846,
     'L2_cond_b_hh': 5.589,
     'L3_cond_bz': 45.051,
     'L3_cond_Wr': 36.7,
     'L3_cond_br': 64.0,
     'L3_cond_bh': 8.0,
     'L3_cond_bp': 8.0}
    for name, (base, spread) in spreads.items():
        noise = np.random.default_rng([zlib.crc32(name.encode()), seed]).standard_normal(out[name].shape)
        drawn = base * np.exp(spread * noise) if base else spread * noise
        out[name] = jnp.asarray(drawn.astype(out[name].dtype))
    for name, factor in factors.items():
        out[name] = (out[name] * factor).astype(out[name].dtype)
    return out
```

```python
import concourse.bass as bass
from concourse import mybir
from contextlib import ExitStack

B, T, D = 2, 2048, 512
P = 128
QUAD = 32
NJ = P // QUAD
KT = D // P
STEPS = QUAD // B
ROWS = STEPS * B
CHUNKS = T // STEPS
PROP = 4
LAG = 2
GROUPS = STEPS // PROP


def cond_resid_kernel(nc, xT, condT, w_rnn_x, w_rnn_h, b_rnn, w_ih, w_hh, b_ih, b_hh,
                      w_rc_x, w_z_x, w_r_h, w_z_h, w_c_h, b_r, b_c, b_z, w_p, b_p, out):
    fp32 = mybir.dt.float32
    ALU = mybir.AluOpType
    ACT = mybir.ActivationFunctionType
    ctx = ExitStack()
    with ctx:
        def sb(name, *free):
            return ctx.enter_context(nc.sbuf_tensor(name, [P, *free], fp32))[:]

        def sem(name):
            return ctx.enter_context(nc.semaphore(name))

        rnn_x = sb("rnn_x", KT, D)
        rnn_h = sb("rnn_h", KT, D)
        ih = sb("ih", KT, D)
        hh = sb("hh", KT, D)
        rc_x = sb("rc_x", KT, NJ, 2 * P)
        z_x = sb("z_x", KT, D)
        r_h = sb("r_h", KT, D)
        z_h = sb("z_h", KT, D)
        c_h = sb("c_h", KT, D)
        prop_w = sb("prop_w", KT, D)
        bias_rnn = sb("bias_rnn", KT)
        bias_ih = sb("bias_ih", KT)
        bias_hh = sb("bias_hh", KT)
        bias_rcz = sb("bias_rcz", 3 * KT)
        bias_p = sb("bias_p", KT)
        cond = sb("cond", KT, B)
        ones = sb("ones", QUAD)
        x_next = sb("x_next", KT, ROWS)
        x_mid = sb("x_mid", KT, ROWS)
        rnn_hist = sb("rnn_hist", KT, ROWS)
        rnn_in_new = sb("rnn_in_new", KT, ROWS)
        rnn_in = sb("rnn_in", KT, ROWS)
        gates_new = sb("gates_new", 3 * KT, ROWS)
        gates_in = sb("gates_in", 3 * KT, ROWS)
        x1 = sb("x1", KT, ROWS)
        qx = sb("qx", KT, ROWS)
        qx_half = sb("qx_half", 2, ROWS)
        qx_sum = sb("qx_sum", ROWS)
        logit = sb("logit", ROWS)
        top = sb("top", STEPS)
        shifted = sb("shifted", ROWS)
        expd = sb("expd", ROWS)
        denom = sb("denom", STEPS)
        inv = sb("inv", STEPS)
        weight = sb("weight", ROWS)
        weight1 = sb("weight1", ROWS)
        x2 = sb("x2", KT, ROWS)
        mid_T = sb("mid_T", KT, ROWS)
        mid_pre = sb("mid_pre", KT, ROWS)
        mid_tanh = sb("mid_tanh", KT, ROWS)
        x3_new = sb("x3_new", KT, ROWS)
        x3 = sb("x3", KT, ROWS)
        y = sb("y", KT, ROWS)
        h_term = sb("h_term", KT, B)
        h_term_a = sb("h_term_a", KT, B)
        h_term_T = sb("h_term_T", KT, QUAD)
        r_T = sb("r_T", KT, QUAD)
        z_T = sb("z_T", KT, QUAD)
        c_T = sb("c_T", KT, QUAD)
        l_T = sb("l_T", KT, QUAD)
        p_T = sb("p_T", KT, QUAD)
        r_pre, z_pre, c_pre, l_pre, p_pre = (sb(n, KT, B) for n in ("r_pre", "z_pre", "c_pre", "l_pre", "p_pre"))
        r_tanh, z_tanh = sb("r_tanh", KT, B), sb("z_tanh", KT, B)
        h_half = sb("h_half", KT, B)
        rh = sb("rh", KT, B)
        one_less_z = sb("one_less_z", KT, B)
        h_prop = sb("h_prop", KT, B)
        scan_mul = sb("scan_mul", KT, B, 2)
        scan_add = sb("scan_add", KT, B, 2)
        gru_hist = sb("gru_hist", STEPS, KT, B, 2)

        def bank(name):
            return ctx.enter_context(nc.psum_tensor(name, [P, 512], fp32))
        ps_r, ps_z, ps_c, ps_l, ps_p, ps_logit, ps_mid, ps_proj = (
            bank(n) for n in ("ps_r", "ps_z", "ps_c", "ps_l", "ps_p", "ps_logit", "ps_mid", "ps_proj"))

        loaded_rnn, loaded_ih, loaded_gru = sem("loaded_rnn"), sem("loaded_ih"), sem("loaded_gru")
        x_next_loaded, x_mid_loaded, stored = sem("x_next_loaded"), sem("x_mid_loaded"), sem("stored")
        banks_clear, ones_set, states_set = sem("banks_clear"), sem("ones_set"), sem("states_set")
        h_term_product, h_term_T_done = sem("h_term_product"), sem("h_term_T_done")
        h_term_a_done, h_term_ready = sem("h_term_a_done"), sem("h_term_ready")
        l_product, l_T_done, l_pre_done, l_ready = (sem(n) for n in ("l_product", "l_T_done", "l_pre_done", "l_ready"))
        r_product, r_T_done, r_pre_done, r_tanh_done = (sem(n) for n in ("r_product", "r_T_done", "r_pre_done", "r_tanh_done"))
        z_product, z_T_done, z_pre_done, z_tanh_done = (sem(n) for n in ("z_product", "z_T_done", "z_pre_done", "z_tanh_done"))
        c_product, c_T_done, c_pre_done, c_tanh_done = (sem(n) for n in ("c_product", "c_T_done", "c_pre_done", "c_tanh_done"))
        h_half_done, rh_ready, z_done, one_less_z_done, kept_done, h_ready = (
            sem(n) for n in ("h_half_done", "rh_ready", "z_done", "one_less_z_done", "kept_done", "h_ready"))
        p_product, p_T_done, p_pre_done, p_ready = (sem(n) for n in ("p_product", "p_T_done", "p_pre_done", "p_ready"))
        x1_done, qx_done, qx_half_done, qx_sum_done = (sem(n) for n in ("x1_done", "qx_done", "qx_half_done", "qx_sum_done"))
        logit_product, logit_done, top_done, shifted_done = (sem(n) for n in ("logit_product", "logit_done", "top_done", "shifted_done"))
        expd_done, denom_done, inv_done, weight_done = (sem(n) for n in ("expd_done", "denom_done", "inv_done", "weight_done"))
        weight1_done, x2_done, mid_product, mid_T_done = (sem(n) for n in ("weight1_done", "x2_done", "mid_product", "mid_T_done"))
        mid_pre_done, mid_tanh_done, x3_new_done, rc_in_product = (sem(n) for n in ("mid_pre_done", "mid_tanh_done", "x3_new_done", "rc_in_product"))
        rc_in_T_done, z_in_product, z_in_T_done, rnn_in_product = (sem(n) for n in ("rc_in_T_done", "z_in_product", "z_in_T_done", "rnn_in_product"))
        rnn_in_T_done, rnn_in_ready, rc_in_ready, z_in_ready = (sem(n) for n in ("rnn_in_T_done", "rnn_in_ready", "rc_in_ready", "z_in_ready"))
        y_ready, x3_ready = sem("y_ready"), sem("x3_ready")

        def after(engine, semaphore, count):
            if not isinstance(count, int) or count > 0:
                engine.wait_ge(semaphore, count)

        def parts(i):
            if not isinstance(i, int):
                return True, True, True, True
            return i < CHUNKS, 1 <= i <= CHUNKS, LAG <= i, i + 1 < CHUNKS

        def last_step(i, u):
            return isinstance(i, int) and i == CHUNKS + LAG - 1 and u == STEPS - 1

        def all_iterations(engine, iteration):
            for i in range(LAG + 1):
                iteration(i)
            with engine.Fori(LAG + 1, CHUNKS - 1) as i:
                iteration(i)
            for i in range(CHUNKS - 1, CHUNKS + LAG):
                iteration(i)

        block = ctx.enter_context(nc.Block())

        @block.sync
        def _(sp):
            sp.dma_start(x_next[:, :, :], xT[0, :, :, :]).then_inc(x_next_loaded, 16)
            for tile, dram in ((rnn_x, w_rnn_x), (cond, condT), (bias_rnn, b_rnn), (rnn_h, w_rnn_h)):
                sp.dma_start(tile, dram).then_inc(loaded_rnn, 16)
            sp.dma_start(x_mid[:, :, :], xT[0, :, :, :]).then_inc(x_mid_loaded, 16)
            for tile, dram in ((hh, w_hh), (bias_ih, b_ih), (bias_hh, b_hh), (ih, w_ih)):
                sp.dma_start(tile, dram).then_inc(loaded_ih, 16)
            for tile, dram in ((rc_x, w_rc_x), (z_x, w_z_x), (bias_rcz[:, 0:KT], b_r), (bias_rcz[:, KT:2 * KT], b_c),
                               (bias_rcz[:, 2 * KT:3 * KT], b_z), (bias_p, b_p), (r_h, w_r_h), (z_h, w_z_h),
                               (c_h, w_c_h), (prop_w, w_p)):
                sp.dma_start(tile, dram).then_inc(loaded_gru, 16)

            def iteration(i):
                rnn, mid, gru, proj = parts(i)
                if proj:
                    sp.wait_ge(rnn_in_product, i + 1)
                    sp.dma_start(x_next[:, :, :], xT[i + 1, :, :, :]).then_inc(x_next_loaded, 16)
                if mid and (not isinstance(i, int) or i < CHUNKS):
                    sp.wait_ge(x1_done, i)
                    sp.dma_start(x_mid[:, :, :], xT[i, :, :, :]).then_inc(x_mid_loaded, 16)
                if gru:
                    sp.wait_ge(y_ready, i - LAG + 1)
                    sp.dma_start(out[i - LAG, :, :, :], y[:, :, :]).then_inc(stored, 16)
            all_iterations(sp, iteration)
            sp.wait_ge(stored, 16 * CHUNKS)

        @block.gpsimd
        def _(pool):
            tt = nc.gpsimd.tensor_tensor
            nc.gpsimd.memset(ones[:, :], 1.0).then_inc(ones_set, 1)

            def bias_rows(bias, blocks):
                return bias.unsqueeze(2).to_broadcast([P, blocks, ROWS])

            def rnn_input(chunk):
                pool.wait_ge(rnn_in_T_done, chunk + 1)
                after(pool, l_pre_done, STEPS * chunk)
                tt(rnn_in[:, :, :], rnn_in_new[:, :, :], bias_rows(bias_rnn[:, :], KT), ALU.add).then_inc(rnn_in_ready, 1)

            pool.wait_ge(loaded_rnn, 16 * 4)
            rnn_input(0)
            pool.wait_ge(loaded_ih, 16 * 4)
            pool.wait_ge(h_term_T_done, 1)
            tt(h_term_a[:, :, :], h_term_T[:, :, 0:B], bias_hh[:, :].unsqueeze(2).to_broadcast([P, KT, B]), ALU.add).then_inc(h_term_a_done, 1)
            pool.wait_ge(h_term_a_done, 1)
            tt(h_term[:, :, :], h_term_a[:, :, :], bias_ih[:, :].unsqueeze(2).to_broadcast([P, KT, B]), ALU.add).then_inc(h_term_ready, 1)
            pool.wait_ge(h_term_ready, 1)
            pool.wait_ge(loaded_gru, 16 * 10)

            def by_time(tile):
                return tile.rearrange("p k (t b) -> p k t b", b=B)

            def iteration(i):
                rnn, mid, gru, proj = parts(i)
                if mid:
                    pool.wait_ge(l_ready, STEPS * i)
                    pool.wait_ge(x_mid_loaded, 16 * i)
                    tt(x1[:, :, :], x_mid[:, :, :], rnn_hist[:, :, :], ALU.add).then_inc(x1_done, 1)
                    pool.wait_ge(x1_done, i)
                    for k in range(KT):
                        last = tt(qx[:, k, :].rearrange("p (t b) -> p t b", b=B), x1[:, k, :].rearrange("p (t b) -> p t b", b=B),
                                  cond[:, k, :].unsqueeze(1).to_broadcast([P, STEPS, B]), ALU.mult)
                    last.then_inc(qx_done, 1)
                    pool.wait_ge(qx_done, i)
                    tt(qx_half[:, :, :], qx[:, 0:2, :], qx[:, 2:4, :], ALU.add).then_inc(qx_half_done, 1)
                    pool.wait_ge(qx_half_done, i)
                    tt(qx_sum[:, :], qx_half[:, 0, :], qx_half[:, 1, :], ALU.add).then_inc(qx_sum_done, 1)
                    pool.wait_ge(top_done, i)
                    pair = logit[:, :].rearrange("p (t b) -> p t b", b=B)
                    tt(shifted[:, :].rearrange("p (t b) -> p t b", b=B), pair, top[:, :].unsqueeze(2).to_broadcast([P, STEPS, B]),
                       ALU.subtract).then_inc(shifted_done, 1)
                    pool.wait_ge(expd_done, i)
                    epair = expd[:, :].rearrange("p (t b) -> p t b", b=B)
                    tt(denom[:, :], epair[:, :, 0], epair[:, :, 1], ALU.add).then_inc(denom_done, 1)
                    pool.wait_ge(inv_done, i)
                    tt(weight[:, :].rearrange("p (t b) -> p t b", b=B), epair, inv[:, :].unsqueeze(2).to_broadcast([P, STEPS, B]),
                       ALU.mult).then_inc(weight_done, 1)
                    pool.wait_ge(weight_done, i)
                    tt(weight1[:, :], weight[:, :], ones[:, :], ALU.add).then_inc(weight1_done, 1)
                    pool.wait_ge(weight1_done, i)
                    tt(x2[:, :, :], x1[:, :, :], weight1[:, :].unsqueeze(1).to_broadcast([P, KT, ROWS]), ALU.mult).then_inc(x2_done, 1)
                    pool.wait_ge(mid_T_done, i)
                    for k in range(KT):
                        last = tt(mid_pre[:, k, :].rearrange("p (t b) -> p t b", b=B), mid_T[:, k, :].rearrange("p (t b) -> p t b", b=B),
                                  h_term[:, k, :].unsqueeze(1).to_broadcast([P, STEPS, B]), ALU.add)
                    last.then_inc(mid_pre_done, 1)
                    pool.wait_ge(mid_tanh_done, i)
                    tt(x3_new[:, :, :], x2[:, :, :], mid_tanh[:, :, :], ALU.add).then_inc(x3_new_done, 1)
                    pool.wait_ge(rc_in_T_done, i)
                    if gru:
                        pool.wait_ge(c_pre_done, STEPS * (i - LAG + 1))
                    tt(gates_in[:, 0:2 * KT, :], gates_new[:, 0:2 * KT, :], bias_rows(bias_rcz[:, 0:2 * KT], 2 * KT), ALU.add).then_inc(rc_in_ready, 1)
                    pool.wait_ge(z_in_T_done, i)
                    tt(gates_in[:, 2 * KT:, :], gates_new[:, 2 * KT:, :], bias_rows(bias_rcz[:, 2 * KT:], KT), ALU.add).then_inc(z_in_ready, 1)
                if gru:
                    pool.wait_ge(h_ready, STEPS * (i - LAG + 1))
                    after(pool, stored, 16 * (i - LAG))
                    for k in range(KT):
                        last = tt(y[:, k, :].rearrange("p (t b) -> p t b", b=B), x3[:, k, :].rearrange("p (t b) -> p t b", b=B),
                                  gru_hist[:, :, k, :, 1], ALU.add)
                    last.then_inc(y_ready, 1)
                    pool.wait_ge(y_ready, i - LAG + 1)
                if mid:
                    tt(x3[:, :, :], x2[:, :, :], mid_tanh[:, :, :], ALU.add).then_inc(x3_ready, 1)
                    pool.wait_ge(x3_ready, i)
                if proj:
                    rnn_input(i + 1)
            all_iterations(pool, iteration)

        @block.tensor
        def _(pe):
            def product(psum, rows, stationary, weights, width=P):
                for k in range(KT):
                    for j in range(NJ):
                        last = nc.tensor.matmul(psum[QUAD * j:QUAD * j + rows, 0:width], stationary(k), weights(k, j),
                                                start=(k == 0), stop=(k == KT - 1))
                return last

            def columns(w):
                return lambda k, j: w[:, k, P * j:P * (j + 1)]

            def project_rnn_input(chunk):
                pe.wait_ge(x_next_loaded, 16 * (chunk + 1))
                after(pe, rnn_in_T_done, chunk)
                product(ps_proj, ROWS, lambda k: x_next[:, k, :], columns(rnn_x)).then_inc(rnn_in_product, 1)

            pe.wait_ge(banks_clear, 1)
            pe.wait_ge(loaded_rnn, 16 * 4)
            project_rnn_input(0)
            pe.wait_ge(loaded_ih, 16 * 4)
            product(ps_mid, B, lambda k: cond[:, k, :], columns(hh)).then_inc(h_term_product, 1)
            pe.wait_ge(states_set, 2)
            pe.wait_ge(ones_set, 1)

            def iteration(i):
                rnn, mid, gru, proj = parts(i)
                for u in range(STEPS):
                    t_rnn = STEPS * i + u
                    t_gru = STEPS * (i - LAG) + u
                    props = GROUPS * (i - LAG) + u // PROP
                    if gru:
                        if u == 0 and isinstance(i, int) is False:
                            pe.wait_ge(loaded_gru, 16 * 10)
                        if u % PROP == 0:
                            pe.wait_ge(p_ready, props)
                            state = lambda k: h_prop[:, k, :]
                        else:
                            pe.wait_ge(h_ready, t_gru)
                            state = lambda k: gru_hist[:, u - 1, k, :, 1]
                        product(ps_r, B, state, columns(r_h)).then_inc(r_product, 1)
                        product(ps_z, B, state, columns(z_h)).then_inc(z_product, 1)
                        pe.wait_ge(rh_ready, t_gru + 1)
                        product(ps_c, B, lambda k: rh[:, k, :], columns(c_h)).then_inc(c_product, 1)
                    if rnn:
                        after(pe, l_ready, t_rnn)
                        at = B * ((u - 1) % STEPS)
                        product(ps_l, B, lambda k: rnn_hist[:, k, at:at + B], columns(rnn_h)).then_inc(l_product, 1)
                    if mid and u == 1:
                        pe.wait_ge(qx_sum_done, i)
                        for j in range(NJ):
                            last = nc.tensor.matmul(ps_logit[QUAD * j:QUAD * (j + 1), 0:ROWS], ones[:, :], qx_sum[:, :], start=True, stop=True)
                        last.then_inc(logit_product, 1)
                    if u % PROP == PROP - 1:
                        if gru and not last_step(i, u):
                            pe.wait_ge(h_ready, t_gru + 1)
                            product(ps_p, B, lambda k: gru_hist[:, u, k, :, 1], columns(prop_w)).then_inc(p_product, 1)
                        if mid and u == PROP - 1:
                            pe.wait_ge(x2_done, i)
                            product(ps_mid, ROWS, lambda k: x2[:, k, :], columns(ih)).then_inc(mid_product, 1)
                        if mid and u == 2 * PROP - 1:
                            pe.wait_ge(x3_new_done, i)
                            product(ps_mid, ROWS, lambda k: x3_new[:, k, :], lambda k, j: rc_x[:, k, j, :], 2 * P).then_inc(rc_in_product, 1)
                        if mid and u == 3 * PROP - 1:
                            pe.wait_ge(rc_in_T_done, i)
                            product(ps_mid, ROWS, lambda k: x3_new[:, k, :], columns(z_x)).then_inc(z_in_product, 1)
                        if proj and u == STEPS - 1:
                            project_rnn_input(i + 1)
            all_iterations(pe, iteration)

        @block.vector
        def _(dve):
            tt = nc.vector.tensor_tensor
            for psum in (ps_r, ps_z, ps_c, ps_l, ps_p, ps_logit, ps_mid, ps_proj):
                last = nc.vector.memset(psum[:, :], 0.0)
            last.then_inc(banks_clear, 1)
            nc.vector.memset(scan_mul[:, :, :, :], 0.0).then_inc(banks_clear, 1)
            dve.wait_ge(banks_clear, 2)

            def transposed(tile, psum, blocks=KT):
                return nc.vector.transpose(tile, psum[:, 0:P * blocks // KT])

            def flat(tile):
                return tile.rearrange("p k r -> p (k r)")

            dve.wait_ge(rnn_in_product, 1)
            transposed(flat(rnn_in_new[:, :, :]), ps_proj).then_inc(rnn_in_T_done, 1)
            dve.wait_ge(loaded_rnn, 16 * 4)
            nc.vector.tensor_copy(rnn_hist[:, :, ROWS - B:ROWS], cond[:, :, :]).then_inc(states_set, 1)
            nc.vector.tensor_copy(h_prop[:, :, :], cond[:, :, :]).then_inc(states_set, 1)
            dve.wait_ge(h_term_product, 1)
            transposed(flat(h_term_T[:, :, :]), ps_mid).then_inc(h_term_T_done, 1)
            dve.wait_ge(states_set, 2)
            dve.wait_ge(loaded_gru, 16 * 10)

            def rnn_pre(i, u):
                t = STEPS * i + u
                dve.wait_ge(l_product, t + 1)
                transposed(flat(l_T[:, :, :]), ps_l).then_inc(l_T_done, 1)
                dve.wait_ge(l_T_done, t + 1)
                if u == 0:
                    dve.wait_ge(rnn_in_ready, i + 1)
                tt(l_pre[:, :, :], l_T[:, :, 0:B], rnn_in[:, :, B * u:B * (u + 1)], ALU.add).then_inc(l_pre_done, 1)

            def iteration(i):
                rnn, mid, gru, proj = parts(i)
                for u in range(STEPS):
                    t = STEPS * (i - LAG) + u
                    props = GROUPS * (i - LAG) + u // PROP
                    rows = slice(B * u, B * (u + 1))
                    if gru:
                        if u % PROP == 0:
                            after(dve, p_ready, props)
                            state = h_prop[:, :, :]
                        else:
                            dve.wait_ge(h_ready, t)
                            state = gru_hist[:, u - 1, :, :, 1]
                        nc.vector.tensor_scalar(h_half[:, :, :], state, 0.5, None, ALU.mult).then_inc(h_half_done, 1)
                    if rnn and u % PROP:
                        rnn_pre(i, u - 1)
                    if mid and u == 2:
                        dve.wait_ge(logit_product, i)
                        nc.vector.tensor_scalar(logit[:, :], ps_logit[:, 0:ROWS], float(D) ** -0.5, None, ALU.mult).then_inc(logit_done, 1)
                        dve.wait_ge(logit_done, i)
                        pair = logit[:, :].rearrange("p (t b) -> p t b", b=B)
                        tt(top[:, :], pair[:, :, 0], pair[:, :, 1], ALU.max).then_inc(top_done, 1)
                    if mid and u == 3:
                        dve.wait_ge(denom_done, i)
                        nc.vector.reciprocal(inv[:, :], denom[:, :]).then_inc(inv_done, 1)
                    if gru:
                        dve.wait_ge(r_product, t + 1)
                        transposed(flat(r_T[:, :, :]), ps_r).then_inc(r_T_done, 1)
                        if u == 0:
                            dve.wait_ge(rc_in_ready, i - 1)
                        dve.wait_ge(r_T_done, t + 1)
                        tt(r_pre[:, :, :], r_T[:, :, 0:B], gates_in[:, 0:KT, rows], ALU.add).then_inc(r_pre_done, 1)
                        dve.wait_ge(h_half_done, t + 1)
                        dve.wait_ge(r_tanh_done, t + 1)
                        nc.vector.scalar_tensor_tensor(rh[:, :, :], r_tanh[:, :, :], 1.0, h_half[:, :, :], ALU.add, ALU.mult).then_inc(rh_ready, 1)
                        dve.wait_ge(z_product, t + 1)
                        transposed(flat(z_T[:, :, :]), ps_z).then_inc(z_T_done, 1)
                        if u == 0:
                            dve.wait_ge(z_in_ready, i - 1)
                        dve.wait_ge(z_T_done, t + 1)
                        tt(z_pre[:, :, :], z_T[:, :, 0:B], gates_in[:, 2 * KT:3 * KT, rows], ALU.add).then_inc(z_pre_done, 1)
                        dve.wait_ge(z_tanh_done, t + 1)
                        nc.vector.tensor_scalar(one_less_z[:, :, :], z_tanh[:, :, :], -0.5, 0.5, ALU.mult, ALU.add).then_inc(one_less_z_done, 1)
                        nc.vector.tensor_scalar(scan_mul[:, :, :, 1], z_tanh[:, :, :], 0.5, 0.5, ALU.mult, ALU.add).then_inc(z_done, 1)
                        dve.wait_ge(one_less_z_done, t + 1)
                        tt(scan_add[:, :, :, 1], one_less_z[:, :, :], state, ALU.mult).then_inc(kept_done, 1)
                        dve.wait_ge(c_product, t + 1)
                        transposed(flat(c_T[:, :, :]), ps_c).then_inc(c_T_done, 1)
                        dve.wait_ge(c_T_done, t + 1)
                        tt(c_pre[:, :, :], c_T[:, :, 0:B], gates_in[:, KT:2 * KT, rows], ALU.add).then_inc(c_pre_done, 1)
                        dve.wait_ge(z_done, t + 1)
                        dve.wait_ge(kept_done, t + 1)
                        if u == 0:
                            after(dve, y_ready, i - LAG)
                        dve.wait_ge(c_tanh_done, t + 1)
                        nc.vector.tensor_tensor_scan(gru_hist[:, u, :, :, :].rearrange("p k b s -> p (k b s)"),
                                                     scan_mul[:, :, :, :].rearrange("p k b s -> p (k b s)"),
                                                     scan_add[:, :, :, :].rearrange("p k b s -> p (k b s)"),
                                                     0.0, ALU.mult, ALU.add).then_inc(h_ready, 1)
                    if u % PROP == PROP - 1:
                        if rnn:
                            rnn_pre(i, u)
                        if gru and not last_step(i, u):
                            dve.wait_ge(p_product, props + 1)
                            transposed(flat(p_T[:, :, :]), ps_p).then_inc(p_T_done, 1)
                            dve.wait_ge(p_T_done, props + 1)
                            tt(p_pre[:, :, :], p_T[:, :, 0:B], bias_p[:, :].unsqueeze(2).to_broadcast([P, KT, B]), ALU.add).then_inc(p_pre_done, 1)
                        if mid and u == PROP - 1:
                            dve.wait_ge(mid_product, i)
                            transposed(flat(mid_T[:, :, :]), ps_mid).then_inc(mid_T_done, 1)
                        if mid and u == 2 * PROP - 1:
                            dve.wait_ge(rc_in_product, i)
                            transposed(flat(gates_new[:, 0:2 * KT, :]), ps_mid, 2 * KT).then_inc(rc_in_T_done, 1)
                        if mid and u == 3 * PROP - 1:
                            dve.wait_ge(z_in_product, i)
                            transposed(flat(gates_new[:, 2 * KT:, :]), ps_mid).then_inc(z_in_T_done, 1)
                        if proj and u == STEPS - 1:
                            dve.wait_ge(rnn_in_product, i + 2)
                            transposed(flat(rnn_in_new[:, :, :]), ps_proj).then_inc(rnn_in_T_done, 1)
            all_iterations(dve, iteration)

        @block.scalar
        def _(act):
            def rnn_tanh(i, u):
                act.wait_ge(l_pre_done, STEPS * i + u + 1)
                if u == 0 and not (isinstance(i, int) and i == 0):
                    act.wait_ge(x1_done, i)
                nc.scalar.activation(rnn_hist[:, :, B * u:B * (u + 1)], l_pre[:, :, :], ACT.Tanh).then_inc(l_ready, 1)

            def iteration(i):
                rnn, mid, gru, proj = parts(i)
                for u in range(STEPS):
                    t = STEPS * (i - LAG) + u
                    props = GROUPS * (i - LAG) + u // PROP
                    if rnn and u % PROP:
                        rnn_tanh(i, u - 1)
                    if mid and u == PROP:
                        act.wait_ge(mid_pre_done, i)
                        nc.scalar.activation(mid_tanh[:, :, :], mid_pre[:, :, :], ACT.Tanh).then_inc(mid_tanh_done, 1)
                    if gru:
                        act.wait_ge(r_pre_done, t + 1)
                        nc.scalar.activation(r_tanh[:, :, :], r_pre[:, :, :], ACT.Tanh, scale=0.5).then_inc(r_tanh_done, 1)
                        act.wait_ge(z_pre_done, t + 1)
                        nc.scalar.activation(z_tanh[:, :, :], z_pre[:, :, :], ACT.Tanh, scale=0.5).then_inc(z_tanh_done, 1)
                        act.wait_ge(c_pre_done, t + 1)
                        nc.scalar.activation(scan_add[:, :, :, 0], c_pre[:, :, :], ACT.Tanh).then_inc(c_tanh_done, 1)
                    if mid and u == 2:
                        act.wait_ge(shifted_done, i)
                        nc.scalar.activation(expd[:, :], shifted[:, :], ACT.Exp).then_inc(expd_done, 1)
                    if u % PROP == PROP - 1:
                        if rnn:
                            rnn_tanh(i, u)
                        if gru and not last_step(i, u):
                            act.wait_ge(p_pre_done, props + 1)
                            nc.scalar.activation(h_prop[:, :, :], p_pre[:, :, :], ACT.Tanh).then_inc(p_ready, 1)
            all_iterations(act, iteration)


def kernel(**inputs):
    import numpy as np
    import concourse.bacc as bacc
    from concourse.bass_utils import run_bass_kernel_spmd

    a = {k: np.asarray(v) for k, v in inputs.items()}

    def by_feature(w):
        rest = w.shape[1:]
        w = w.reshape(NJ, KT, QUAD, *rest)
        return np.ascontiguousarray(np.swapaxes(w, 1, 2).reshape(P, KT, *rest))

    Wr, Wz, Wh = a["L3_cond_Wr"], a["L3_cond_Wz"], a["L3_cond_Wh"]
    rc = np.stack([Wr[:D].reshape(D, NJ, P), Wh[:D].reshape(D, NJ, P)], axis=2).reshape(D, NJ, 2 * P)
    x = a["x"].reshape(B, CHUNKS, STEPS, NJ, KT, QUAD).transpose(1, 3, 5, 4, 2, 0)
    x = np.ascontiguousarray(x.reshape(CHUNKS, P, KT, ROWS))
    arrays = {
        "xT": x, "condT": by_feature(a["cond_1024"].T),
        "w_rnn_x": by_feature(a["L0_cond_Wx"]), "w_rnn_h": by_feature(a["L0_cond_Wh"]), "b_rnn": by_feature(a["L0_cond_b"]),
        "w_ih": by_feature(a["L2_cond_W_ih"].T), "w_hh": by_feature(a["L2_cond_W_hh"].T),
        "b_ih": by_feature(a["L2_cond_b_ih"]), "b_hh": by_feature(a["L2_cond_b_hh"]),
        "w_rc_x": by_feature(rc), "w_z_x": by_feature(Wz[:D]),
        "w_r_h": by_feature(Wr[D:]), "w_z_h": by_feature(Wz[D:]), "w_c_h": by_feature(Wh[D:]),
        "b_r": by_feature(a["L3_cond_br"]), "b_c": by_feature(a["L3_cond_bh"]), "b_z": by_feature(a["L3_cond_bz"]),
        "w_p": by_feature(a["L3_cond_Wp"]), "b_p": by_feature(a["L3_cond_bp"]),
    }
    nc = bacc.Bacc("TRN2", target_bir_lowering=False, num_devices=1)
    args = [nc.dram_tensor(name, v.shape, mybir.dt.from_np(v.dtype), kind="ExternalInput").ap() for name, v in arrays.items()]
    args.append(nc.dram_tensor("y_out", (CHUNKS, P, KT, ROWS), mybir.dt.float32, kind="ExternalOutput").ap())
    cond_resid_kernel(nc, *args)
    got = run_bass_kernel_spmd(nc, [arrays], core_ids=[0]).results[0]["y_out"]
    got = got.reshape(CHUNKS, NJ, QUAD, KT, STEPS, B).transpose(5, 0, 4, 1, 3, 2)
    return np.ascontiguousarray(got.reshape(B, T, D))
```

```python
import concourse.bass as bass
from concourse import mybir
from contextlib import ExitStack

B, T, D = 2, 2048, 512
P = 128
QUAD = 32
NJ = P // QUAD
KT = D // P
STEPS = QUAD // B
ROWS = STEPS * B
CHUNKS = T // STEPS
PROP = 4
LAG = 2
GROUPS = STEPS // PROP
HALF = STEPS // 2


def cond_resid_kernel(nc, xT, condT, w_rnn_x, w_rnn_h, b_rnn, w_ih, w_hh, b_ih, b_hh,
                      w_rc_x, w_z_x, w_r_h, w_z_h, w_c_h, b_rcz, w_p, b_p, rnn_spill, gates_spill, out):
    fp32 = mybir.dt.float32
    ALU = mybir.AluOpType
    ACT = mybir.ActivationFunctionType
    ctx = ExitStack()
    with ctx:
        def sb(name, *free):
            return ctx.enter_context(nc.sbuf_tensor(name, [P, *free], fp32))[:]

        def sem(name):
            return ctx.enter_context(nc.semaphore(name))

        rnn_x = sb("rnn_x", KT, D)
        rnn_h = sb("rnn_h", KT, D)
        ih = sb("ih", KT, D)
        hh = sb("hh", KT, D)
        rc_x = sb("rc_x", KT, NJ, 2 * P)
        z_x = sb("z_x", KT, D)
        r_h = sb("r_h", KT, D)
        z_h = sb("z_h", KT, D)
        c_h = sb("c_h", KT, D)
        prop_w = sb("prop_w", KT, D)
        bias_ih = sb("bias_ih", KT)
        bias_hh = sb("bias_hh", KT)
        bias_rnn = sb("bias_rnn", P)
        bias_rcz = sb("bias_rcz", 3, P)
        bias_p = sb("bias_p", P)
        zeros = sb("zeros", QUAD)
        cond = sb("cond", KT, B)
        ones = sb("ones", QUAD)
        x_next = sb("x_next", KT, ROWS)
        x_mid = sb("x_mid", KT, ROWS)
        rnn_hist = sb("rnn_hist", KT, ROWS)
        rnn_rows = sb("rnn_rows", P)
        gates_rows = sb("gates_rows", 3, P)
        rnn_seeds = sb("rnn_seeds", STEPS, P)
        gates_seeds = sb("gates_seeds", STEPS, 3, P)
        x1 = sb("x1", KT, ROWS)
        qx = sb("qx", KT, ROWS)
        qx_half = sb("qx_half", 2, ROWS)
        qx_sum = sb("qx_sum", ROWS)
        logit = sb("logit", ROWS)
        top = sb("top", STEPS)
        shifted = sb("shifted", ROWS)
        expd = sb("expd", ROWS)
        denom = sb("denom", STEPS)
        inv = sb("inv", STEPS)
        weight = sb("weight", ROWS)
        weight1 = sb("weight1", ROWS)
        x2 = sb("x2", KT, ROWS)
        mid_T = sb("mid_T", KT, ROWS)
        mid_pre = sb("mid_pre", KT, ROWS)
        mid_tanh = sb("mid_tanh", KT, ROWS)
        x3_new = sb("x3_new", KT, ROWS)
        x3 = sb("x3", KT, ROWS)
        y = sb("y", KT, ROWS)
        h_term = sb("h_term", KT, B)
        h_term_a = sb("h_term_a", KT, B)
        h_term_T = sb("h_term_T", KT, QUAD)
        r_T = sb("r_T", KT, QUAD)
        z_T = sb("z_T", KT, QUAD)
        c_T = sb("c_T", KT, QUAD)
        l_T = sb("l_T", KT, QUAD)
        p_T = sb("p_T", KT, QUAD)
        r_tanh, z_tanh = sb("r_tanh", KT, B), sb("z_tanh", KT, B)
        h_half = sb("h_half", KT, B)
        rh = sb("rh", KT, B)
        one_less_z = sb("one_less_z", KT, B)
        h_prop = sb("h_prop", KT, B)
        scan_mul = sb("scan_mul", KT, B, 2)
        scan_add = sb("scan_add", KT, B, 2)
        gru_hist = sb("gru_hist", STEPS, KT, B, 2)

        def bank(name):
            return ctx.enter_context(nc.psum_tensor(name, [P, 512], fp32))
        ps_r, ps_z, ps_c, ps_l, ps_p, ps_logit, ps_mid, ps_proj = (
            bank(n) for n in ("ps_r", "ps_z", "ps_c", "ps_l", "ps_p", "ps_logit", "ps_mid", "ps_proj"))

        loaded_rnn, loaded_ih, loaded_gru = sem("loaded_rnn"), sem("loaded_ih"), sem("loaded_gru")
        x_next_loaded, x_mid_loaded, stored = sem("x_next_loaded"), sem("x_mid_loaded"), sem("stored")
        banks_clear, banks_open, ones_set, states_set = sem("banks_clear"), sem("banks_open"), sem("ones_set"), sem("states_set")
        h_term_product, h_term_T_done = sem("h_term_product"), sem("h_term_T_done")
        h_term_a_done, h_term_ready = sem("h_term_a_done"), sem("h_term_ready")
        l_seeded, l_product, l_T_done, l_ready = (sem(n) for n in ("l_seeded", "l_product", "l_T_done", "l_ready"))
        r_seeded, r_product, r_T_done, r_tanh_done = (sem(n) for n in ("r_seeded", "r_product", "r_T_done", "r_tanh_done"))
        z_seeded, z_product, z_T_done, z_tanh_done = (sem(n) for n in ("z_seeded", "z_product", "z_T_done", "z_tanh_done"))
        c_seeded, c_product, c_T_done, c_tanh_done = (sem(n) for n in ("c_seeded", "c_product", "c_T_done", "c_tanh_done"))
        h_half_done, rh_ready, z_done, one_less_z_done, kept_done, h_ready = (
            sem(n) for n in ("h_half_done", "rh_ready", "z_done", "one_less_z_done", "kept_done", "h_ready"))
        p_seeded, p_product, p_T_done, p_ready = (sem(n) for n in ("p_seeded", "p_product", "p_T_done", "p_ready"))
        x1_done, qx_done, qx_half_done, qx_sum_done = (sem(n) for n in ("x1_done", "qx_done", "qx_half_done", "qx_sum_done"))
        logit_product, logit_done, top_done, shifted_done = (sem(n) for n in ("logit_product", "logit_done", "top_done", "shifted_done"))
        expd_done, denom_done, inv_done, weight_done = (sem(n) for n in ("expd_done", "denom_done", "inv_done", "weight_done"))
        weight1_done, x2_done, mid_product, mid_T_done = (sem(n) for n in ("weight1_done", "x2_done", "mid_product", "mid_T_done"))
        mid_pre_done, mid_tanh_done, x3_new_done, rc_in_product = (sem(n) for n in ("mid_pre_done", "mid_tanh_done", "x3_new_done", "rc_in_product"))
        rc_rows_done, z_in_product, z_rows_done = (sem(n) for n in ("rc_rows_done", "z_in_product", "z_rows_done"))
        rnn_in_product, rnn_rows_done = sem("rnn_in_product"), sem("rnn_rows_done")
        rnn_spilled, gates_spilled, seeds_clear = sem("rnn_spilled"), sem("gates_spilled"), sem("seeds_clear")
        rnn_fetched = [sem("rnn_fetched_0"), sem("rnn_fetched_1")]
        gates_fetched = [sem("gates_fetched_0"), sem("gates_fetched_1")]
        y_ready, x3_ready = sem("y_ready"), sem("x3_ready")

        def after(engine, semaphore, count):
            if not isinstance(count, int) or count > 0:
                engine.wait_ge(semaphore, count)

        def parts(i):
            if not isinstance(i, int):
                return True, True, True, True
            return i < CHUNKS, 1 <= i <= CHUNKS, LAG <= i, i + 2 < CHUNKS

        def next_rnn(i):
            return not isinstance(i, int) or i + 1 < CHUNKS

        def next_gru(i):
            return not isinstance(i, int) or LAG <= i + 1 < CHUNKS + LAG

        def last_step(i, u):
            return isinstance(i, int) and i == CHUNKS + LAG - 1 and u == STEPS - 1

        def all_iterations(engine, iteration):
            for i in range(LAG + 1):
                iteration(i)
            with engine.Fori(LAG + 1, CHUNKS - 2) as i:
                iteration(i)
            for i in range(CHUNKS - 2, CHUNKS + LAG):
                iteration(i)

        block = ctx.enter_context(nc.Block())

        @block.sync
        def _(sp):
            sp.dma_start(x_next[:, :, :], xT[0, :, :, :]).then_inc(x_next_loaded, 16)
            for tile, dram in ((rnn_x, w_rnn_x), (bias_rnn, b_rnn), (cond, condT), (rnn_h, w_rnn_h)):
                sp.dma_start(tile, dram).then_inc(loaded_rnn, 16)
            sp.dma_start(x_mid[:, :, :], xT[0, :, :, :]).then_inc(x_mid_loaded, 16)
            for tile, dram in ((hh, w_hh), (bias_ih, b_ih), (bias_hh, b_hh), (ih, w_ih)):
                sp.dma_start(tile, dram).then_inc(loaded_ih, 16)

            def spill_rnn(chunk):
                sp.wait_ge(rnn_rows_done, chunk + 1)
                for half in range(2):
                    after(sp, rnn_fetched[half], 16 * B * chunk)
                sp.dma_start(rnn_spill, rnn_rows[:, :]).then_inc(rnn_spilled, 16)

            def fetch_rnn(chunk, half):
                steps = slice(HALF * half, HALF * (half + 1))
                sp.wait_ge(rnn_spilled, 16 * (chunk + 1))
                after(sp, l_seeded, STEPS * chunk - STEPS + HALF * (half + 1))
                for b in range(B):
                    sp.dma_start(rnn_seeds[b:P:QUAD, steps, :], rnn_spill.rearrange("(j t b) n -> j t b n", j=NJ, b=B)[:, steps, b, :])\
                      .then_inc(rnn_fetched[half], 16)

            def fetch_gates(chunk, half):
                steps = slice(HALF * half, HALF * (half + 1))
                sp.wait_ge(gates_spilled, 16 * (chunk + 1))
                for seeded in (r_seeded, z_seeded, c_seeded):
                    after(sp, seeded, STEPS * chunk - STEPS + HALF * (half + 1))
                for b in range(B):
                    sp.dma_start(gates_seeds[b:P:QUAD, steps, :, :],
                                 gates_spill.rearrange("(j t b) g n -> j t b g n", j=NJ, b=B)[:, steps, b, :, :])\
                      .then_inc(gates_fetched[half], 16)

            sp.wait_ge(rnn_in_product, 1)
            sp.dma_start(x_next[:, :, :], xT[1, :, :, :]).then_inc(x_next_loaded, 16)
            sp.wait_ge(seeds_clear, 3)
            spill_rnn(0)
            fetch_rnn(0, 0)
            fetch_rnn(0, 1)
            for tile, dram in ((rc_x, w_rc_x), (z_x, w_z_x), (bias_rcz, b_rcz), (bias_p, b_p), (r_h, w_r_h), (z_h, w_z_h),
                               (c_h, w_c_h), (prop_w, w_p)):
                sp.dma_start(tile, dram).then_inc(loaded_gru, 16)

            def iteration(i):
                rnn, mid, gru, proj = parts(i)
                if proj:
                    sp.wait_ge(rnn_in_product, i + 2)
                    sp.dma_start(x_next[:, :, :], xT[i + 2, :, :, :]).then_inc(x_next_loaded, 16)
                if mid and (not isinstance(i, int) or i < CHUNKS):
                    sp.wait_ge(x1_done, i)
                    sp.dma_start(x_mid[:, :, :], xT[i, :, :, :]).then_inc(x_mid_loaded, 16)
                if next_rnn(i):
                    spill_rnn(i + 1)
                    fetch_rnn(i + 1, 0)
                if mid:
                    sp.wait_ge(rc_rows_done, i)
                    sp.wait_ge(z_rows_done, i)
                    for half in range(2):
                        after(sp, gates_fetched[half], 16 * B * (i - 1))
                    sp.dma_start(gates_spill, gates_rows[:, :, :]).then_inc(gates_spilled, 16)
                    fetch_gates(i - 1, 0)
                    fetch_gates(i - 1, 1)
                if next_rnn(i):
                    fetch_rnn(i + 1, 1)
                if gru:
                    sp.wait_ge(y_ready, i - LAG + 1)
                    sp.dma_start(out[i - LAG, :, :, :], y[:, :, :]).then_inc(stored, 16)
            all_iterations(sp, iteration)
            sp.wait_ge(stored, 16 * CHUNKS)

        @block.gpsimd
        def _(pool):
            tt = nc.gpsimd.tensor_tensor
            nc.gpsimd.memset(ones[:, :], 1.0).then_inc(ones_set, 1)

            nc.gpsimd.memset(rnn_seeds[:, :, :], 0.0).then_inc(seeds_clear, 1)
            nc.gpsimd.memset(gates_seeds[:, :, :, :], 0.0).then_inc(seeds_clear, 1)
            nc.gpsimd.memset(zeros[:, :], 0.0).then_inc(seeds_clear, 1)
            pool.wait_ge(loaded_rnn, 16 * 4)
            pool.wait_ge(loaded_ih, 16 * 4)
            pool.wait_ge(h_term_T_done, 1)
            tt(h_term_a[:, :, :], h_term_T[:, :, 0:B], bias_hh[:, :].unsqueeze(2).to_broadcast([P, KT, B]), ALU.add).then_inc(h_term_a_done, 1)
            pool.wait_ge(h_term_a_done, 1)
            tt(h_term[:, :, :], h_term_a[:, :, :], bias_ih[:, :].unsqueeze(2).to_broadcast([P, KT, B]), ALU.add).then_inc(h_term_ready, 1)
            pool.wait_ge(h_term_ready, 1)
            def by_time(tile):
                return tile.rearrange("p k (t b) -> p k t b", b=B)

            def iteration(i):
                rnn, mid, gru, proj = parts(i)
                if mid:
                    pool.wait_ge(l_ready, STEPS * i)
                    pool.wait_ge(x_mid_loaded, 16 * i)
                    tt(x1[:, :, :], x_mid[:, :, :], rnn_hist[:, :, :], ALU.add).then_inc(x1_done, 1)
                    pool.wait_ge(x1_done, i)
                    for k in range(KT):
                        last = tt(qx[:, k, :].rearrange("p (t b) -> p t b", b=B), x1[:, k, :].rearrange("p (t b) -> p t b", b=B),
                                  cond[:, k, :].unsqueeze(1).to_broadcast([P, STEPS, B]), ALU.mult)
                    last.then_inc(qx_done, 1)
                    pool.wait_ge(qx_done, i)
                    tt(qx_half[:, :, :], qx[:, 0:2, :], qx[:, 2:4, :], ALU.add).then_inc(qx_half_done, 1)
                    pool.wait_ge(qx_half_done, i)
                    tt(qx_sum[:, :], qx_half[:, 0, :], qx_half[:, 1, :], ALU.add).then_inc(qx_sum_done, 1)
                    pool.wait_ge(top_done, i)
                    pair = logit[:, :].rearrange("p (t b) -> p t b", b=B)
                    tt(shifted[:, :].rearrange("p (t b) -> p t b", b=B), pair, top[:, :].unsqueeze(2).to_broadcast([P, STEPS, B]),
                       ALU.subtract).then_inc(shifted_done, 1)
                    pool.wait_ge(expd_done, i)
                    epair = expd[:, :].rearrange("p (t b) -> p t b", b=B)
                    tt(denom[:, :], epair[:, :, 0], epair[:, :, 1], ALU.add).then_inc(denom_done, 1)
                    pool.wait_ge(inv_done, i)
                    tt(weight[:, :].rearrange("p (t b) -> p t b", b=B), epair, inv[:, :].unsqueeze(2).to_broadcast([P, STEPS, B]),
                       ALU.mult).then_inc(weight_done, 1)
                    pool.wait_ge(weight_done, i)
                    tt(weight1[:, :], weight[:, :], ones[:, :], ALU.add).then_inc(weight1_done, 1)
                    pool.wait_ge(weight1_done, i)
                    tt(x2[:, :, :], x1[:, :, :], weight1[:, :].unsqueeze(1).to_broadcast([P, KT, ROWS]), ALU.mult).then_inc(x2_done, 1)
                    pool.wait_ge(mid_T_done, i)
                    for k in range(KT):
                        last = tt(mid_pre[:, k, :].rearrange("p (t b) -> p t b", b=B), mid_T[:, k, :].rearrange("p (t b) -> p t b", b=B),
                                  h_term[:, k, :].unsqueeze(1).to_broadcast([P, STEPS, B]), ALU.add)
                    last.then_inc(mid_pre_done, 1)
                    pool.wait_ge(mid_tanh_done, i)
                    tt(x3_new[:, :, :], x2[:, :, :], mid_tanh[:, :, :], ALU.add).then_inc(x3_new_done, 1)
                if gru:
                    pool.wait_ge(h_ready, STEPS * (i - LAG + 1))
                    after(pool, stored, 16 * (i - LAG))
                    for k in range(KT):
                        last = tt(y[:, k, :].rearrange("p (t b) -> p t b", b=B), x3[:, k, :].rearrange("p (t b) -> p t b", b=B),
                                  gru_hist[:, :, k, :, 1], ALU.add)
                    last.then_inc(y_ready, 1)
                    pool.wait_ge(y_ready, i - LAG + 1)
                if mid:
                    tt(x3[:, :, :], x2[:, :, :], mid_tanh[:, :, :], ALU.add).then_inc(x3_ready, 1)
                    pool.wait_ge(x3_ready, i)
            all_iterations(pool, iteration)

        @block.tensor
        def _(pe):
            def product(psum, rows, stationary, weights, width=P):
                for k in range(KT):
                    for j in range(NJ):
                        last = nc.tensor.matmul(psum[QUAD * j:QUAD * j + rows, 0:width], stationary(k), weights(k, j),
                                                start=(k == 0), stop=(k == KT - 1))
                return last

            def seeded_product(psum, stationary, w):
                for k in range(KT):
                    for j in range(NJ):
                        last = nc.tensor.matmul(psum[QUAD * j:QUAD * j + B, 0:P], stationary(k), w[:, k, P * j:P * (j + 1)],
                                                start=False, stop=(k == KT - 1), skip_group_check=True)
                return last

            def open_bank(psum):
                for j in range(NJ):
                    last = nc.tensor.matmul(psum[QUAD * j:QUAD * (j + 1), 0:P], zeros[:, :], rnn_x[:, 0, 0:P], start=True, stop=True)
                return last

            def columns(w):
                return lambda k, j: w[:, k, P * j:P * (j + 1)]

            def project_rnn_input(chunk):
                pe.wait_ge(x_next_loaded, 16 * (chunk + 1))
                after(pe, rnn_rows_done, chunk)
                product(ps_proj, ROWS, lambda k: x_next[:, k, :], columns(rnn_x)).then_inc(rnn_in_product, 1)

            pe.wait_ge(banks_clear, 1)
            pe.wait_ge(loaded_rnn, 16 * 4)
            project_rnn_input(0)
            pe.wait_ge(seeds_clear, 3)
            for psum in (ps_l, ps_p, ps_r, ps_z, ps_c):
                open_bank(psum).then_inc(banks_open, 1)
            project_rnn_input(1)
            pe.wait_ge(loaded_ih, 16 * 4)
            product(ps_mid, B, lambda k: cond[:, k, :], columns(hh)).then_inc(h_term_product, 1)
            pe.wait_ge(states_set, 2)
            pe.wait_ge(ones_set, 1)

            def iteration(i):
                rnn, mid, gru, proj = parts(i)
                if isinstance(i, int) and i == 1:
                    pe.wait_ge(loaded_gru, 16 * 8)
                for u in range(STEPS):
                    t_rnn = STEPS * i + u
                    t_gru = STEPS * (i - LAG) + u
                    props = GROUPS * (i - LAG) + u // PROP
                    if gru:
                        if u % PROP == 0:
                            pe.wait_ge(p_ready, props)
                            state = lambda k: h_prop[:, k, :]
                        else:
                            pe.wait_ge(h_ready, t_gru)
                            state = lambda k: gru_hist[:, u - 1, k, :, 1]
                        pe.wait_ge(r_seeded, t_gru + 1)
                        seeded_product(ps_r, state, r_h).then_inc(r_product, 1)
                        pe.wait_ge(z_seeded, t_gru + 1)
                        seeded_product(ps_z, state, z_h).then_inc(z_product, 1)
                        pe.wait_ge(c_seeded, t_gru + 1)
                        pe.wait_ge(rh_ready, t_gru + 1)
                        seeded_product(ps_c, lambda k: rh[:, k, :], c_h).then_inc(c_product, 1)
                    if rnn:
                        after(pe, l_ready, t_rnn)
                        at = B * ((u - 1) % STEPS)
                        pe.wait_ge(l_seeded, t_rnn + 1)
                        seeded_product(ps_l, lambda k: rnn_hist[:, k, at:at + B], rnn_h).then_inc(l_product, 1)
                    if mid and u == 1:
                        pe.wait_ge(qx_sum_done, i)
                        for j in range(NJ):
                            last = nc.tensor.matmul(ps_logit[QUAD * j:QUAD * (j + 1), 0:ROWS], ones[:, :], qx_sum[:, :], start=True, stop=True)
                        last.then_inc(logit_product, 1)
                    if u % PROP == PROP - 1:
                        if gru and not last_step(i, u):
                            pe.wait_ge(h_ready, t_gru + 1)
                            pe.wait_ge(p_seeded, props + 1)
                            seeded_product(ps_p, lambda k: gru_hist[:, u, k, :, 1], prop_w).then_inc(p_product, 1)
                        if mid and u == PROP - 1:
                            pe.wait_ge(x2_done, i)
                            product(ps_mid, ROWS, lambda k: x2[:, k, :], columns(ih)).then_inc(mid_product, 1)
                        if mid and u == 2 * PROP - 1:
                            pe.wait_ge(x3_new_done, i)
                            product(ps_mid, ROWS, lambda k: x3_new[:, k, :], lambda k, j: rc_x[:, k, j, :], 2 * P).then_inc(rc_in_product, 1)
                        if mid and u == 3 * PROP - 1:
                            pe.wait_ge(rc_rows_done, i)
                            product(ps_mid, ROWS, lambda k: x3_new[:, k, :], columns(z_x)).then_inc(z_in_product, 1)
                        if proj and u == STEPS - 1:
                            project_rnn_input(i + 2)
            all_iterations(pe, iteration)

        @block.vector
        def _(dve):
            tt = nc.vector.tensor_tensor
            for psum in (ps_r, ps_z, ps_c, ps_l, ps_p, ps_logit, ps_mid, ps_proj):
                last = nc.vector.memset(psum[:, :], 0.0)
            last.then_inc(banks_clear, 1)
            nc.vector.memset(scan_mul[:, :, :, :], 0.0).then_inc(banks_clear, 1)
            dve.wait_ge(banks_clear, 2)

            def transposed(tile, psum):
                return nc.vector.transpose(tile, psum[:, 0:P])

            def flat(tile):
                return tile.rearrange("p k r -> p (k r)")

            def rnn_input_rows(chunk):
                dve.wait_ge(rnn_in_product, chunk + 1)
                after(dve, rnn_spilled, 16 * chunk)
                tt(rnn_rows[:, :], ps_proj[:, 0:P], bias_rnn[:, :], ALU.add).then_inc(rnn_rows_done, 1)

            dve.wait_ge(loaded_rnn, 16 * 4)
            rnn_input_rows(0)
            nc.vector.tensor_copy(rnn_hist[:, :, ROWS - B:ROWS], cond[:, :, :]).then_inc(states_set, 1)
            nc.vector.tensor_copy(h_prop[:, :, :], cond[:, :, :]).then_inc(states_set, 1)
            dve.wait_ge(h_term_product, 1)
            transposed(flat(h_term_T[:, :, :]), ps_mid).then_inc(h_term_T_done, 1)
            rnn_input_rows(1)
            dve.wait_ge(states_set, 2)

            def rnn_T(i, u):
                dve.wait_ge(l_product, STEPS * i + u + 1)
                transposed(flat(l_T[:, :, :]), ps_l).then_inc(l_T_done, 1)

            def iteration(i):
                rnn, mid, gru, proj = parts(i)
                for u in range(STEPS):
                    t = STEPS * (i - LAG) + u
                    props = GROUPS * (i - LAG) + u // PROP
                    if gru:
                        if u % PROP == 0:
                            after(dve, p_ready, props)
                            state = h_prop[:, :, :]
                        else:
                            dve.wait_ge(h_ready, t)
                            state = gru_hist[:, u - 1, :, :, 1]
                        nc.vector.tensor_scalar(h_half[:, :, :], state, 0.5, None, ALU.mult).then_inc(h_half_done, 1)
                    if rnn and u % PROP:
                        rnn_T(i, u - 1)
                    if mid and u == 2:
                        dve.wait_ge(logit_product, i)
                        nc.vector.tensor_scalar(logit[:, :], ps_logit[:, 0:ROWS], float(D) ** -0.5, None, ALU.mult).then_inc(logit_done, 1)
                        dve.wait_ge(logit_done, i)
                        pair = logit[:, :].rearrange("p (t b) -> p t b", b=B)
                        tt(top[:, :], pair[:, :, 0], pair[:, :, 1], ALU.max).then_inc(top_done, 1)
                    if mid and u == 3:
                        dve.wait_ge(denom_done, i)
                        nc.vector.reciprocal(inv[:, :], denom[:, :]).then_inc(inv_done, 1)
                    if gru:
                        dve.wait_ge(r_product, t + 1)
                        transposed(flat(r_T[:, :, :]), ps_r).then_inc(r_T_done, 1)
                        dve.wait_ge(h_half_done, t + 1)
                        dve.wait_ge(r_tanh_done, t + 1)
                        nc.vector.scalar_tensor_tensor(rh[:, :, :], r_tanh[:, :, :], 1.0, h_half[:, :, :], ALU.add, ALU.mult).then_inc(rh_ready, 1)
                        dve.wait_ge(z_product, t + 1)
                        transposed(flat(z_T[:, :, :]), ps_z).then_inc(z_T_done, 1)
                        dve.wait_ge(z_tanh_done, t + 1)
                        nc.vector.tensor_scalar(one_less_z[:, :, :], z_tanh[:, :, :], -0.5, 0.5, ALU.mult, ALU.add).then_inc(one_less_z_done, 1)
                        nc.vector.tensor_scalar(scan_mul[:, :, :, 1], z_tanh[:, :, :], 0.5, 0.5, ALU.mult, ALU.add).then_inc(z_done, 1)
                        dve.wait_ge(one_less_z_done, t + 1)
                        tt(scan_add[:, :, :, 1], one_less_z[:, :, :], state, ALU.mult).then_inc(kept_done, 1)
                        dve.wait_ge(c_product, t + 1)
                        transposed(flat(c_T[:, :, :]), ps_c).then_inc(c_T_done, 1)
                        dve.wait_ge(z_done, t + 1)
                        dve.wait_ge(kept_done, t + 1)
                        if u == 0:
                            after(dve, y_ready, i - LAG)
                        dve.wait_ge(c_tanh_done, t + 1)
                        nc.vector.tensor_tensor_scan(gru_hist[:, u, :, :, :].rearrange("p k b s -> p (k b s)"),
                                                     scan_mul[:, :, :, :].rearrange("p k b s -> p (k b s)"),
                                                     scan_add[:, :, :, :].rearrange("p k b s -> p (k b s)"),
                                                     0.0, ALU.mult, ALU.add).then_inc(h_ready, 1)
                    if u % PROP == PROP - 1:
                        if rnn:
                            rnn_T(i, u)
                        if gru and not last_step(i, u):
                            dve.wait_ge(p_product, props + 1)
                            transposed(flat(p_T[:, :, :]), ps_p).then_inc(p_T_done, 1)
                        if mid and u == PROP - 1:
                            dve.wait_ge(mid_product, i)
                            transposed(flat(mid_T[:, :, :]), ps_mid).then_inc(mid_T_done, 1)
                        if mid and u == 2 * PROP - 1:
                            dve.wait_ge(rc_in_product, i)
                            if isinstance(i, int) and i == 1:
                                dve.wait_ge(loaded_gru, 16 * 8)
                            after(dve, gates_spilled, 16 * (i - 1))
                            tt(gates_rows[:, 0:2, :].rearrange("p g n -> p (g n)"), ps_mid[:, 0:2 * P],
                               bias_rcz[:, 0:2, :].rearrange("p g n -> p (g n)"), ALU.add).then_inc(rc_rows_done, 1)
                        if mid and u == 3 * PROP - 1:
                            dve.wait_ge(z_in_product, i)
                            tt(gates_rows[:, 2, :], ps_mid[:, 0:P], bias_rcz[:, 2, :], ALU.add).then_inc(z_rows_done, 1)
                        if proj and u == STEPS - 1:
                            rnn_input_rows(i + 2)
            all_iterations(dve, iteration)

        @block.scalar
        def _(act):
            def seed(psum, rows):
                return nc.scalar.activation(psum[:, 0:P], rows, ACT.Copy)

            def seed_rnn(i, u):
                if u % HALF == 0:
                    act.wait_ge(rnn_fetched[u // HALF], 16 * B * (i + 1))
                after(act, l_T_done, STEPS * i + u)
                seed(ps_l, rnn_seeds[:, u, :]).then_inc(l_seeded, 1)

            def seed_gate(i, u, gate, psum, T_done, seeded):
                if u % HALF == 0:
                    act.wait_ge(gates_fetched[u // HALF], 16 * B * (i - LAG + 1))
                after(act, T_done, STEPS * (i - LAG) + u)
                seed(psum, gates_seeds[:, u, gate, :]).then_inc(seeded, 1)

            def seed_next_gate(i, u, gate, psum, T_done, seeded):
                if u < STEPS - 1:
                    seed_gate(i, u + 1, gate, psum, T_done, seeded)
                elif next_gru(i):
                    seed_gate(i + 1, 0, gate, psum, T_done, seeded)

            def rnn_tanh(i, u):
                act.wait_ge(l_T_done, STEPS * i + u + 1)
                if u == 0 and not (isinstance(i, int) and i == 0):
                    act.wait_ge(x1_done, i)
                nc.scalar.activation(rnn_hist[:, :, B * u:B * (u + 1)], l_T[:, :, 0:B], ACT.Tanh).then_inc(l_ready, 1)
                if u < STEPS - 1:
                    seed_rnn(i, u + 1)
                elif next_rnn(i):
                    seed_rnn(i + 1, 0)

            act.wait_ge(banks_open, 5)
            act.wait_ge(states_set, 2)
            seed_rnn(0, 0)

            def iteration(i):
                rnn, mid, gru, proj = parts(i)
                for u in range(STEPS):
                    t = STEPS * (i - LAG) + u
                    props = GROUPS * (i - LAG) + u // PROP
                    if rnn and u % PROP:
                        rnn_tanh(i, u - 1)
                    if mid and u == PROP:
                        act.wait_ge(mid_pre_done, i)
                        nc.scalar.activation(mid_tanh[:, :, :], mid_pre[:, :, :], ACT.Tanh).then_inc(mid_tanh_done, 1)
                    if gru:
                        act.wait_ge(r_T_done, t + 1)
                        nc.scalar.activation(r_tanh[:, :, :], r_T[:, :, 0:B], ACT.Tanh, scale=0.5).then_inc(r_tanh_done, 1)
                        seed_next_gate(i, u, 0, ps_r, r_T_done, r_seeded)
                        act.wait_ge(z_T_done, t + 1)
                        nc.scalar.activation(z_tanh[:, :, :], z_T[:, :, 0:B], ACT.Tanh, scale=0.5).then_inc(z_tanh_done, 1)
                        seed_next_gate(i, u, 2, ps_z, z_T_done, z_seeded)
                        act.wait_ge(c_T_done, t + 1)
                        nc.scalar.activation(scan_add[:, :, :, 0], c_T[:, :, 0:B], ACT.Tanh).then_inc(c_tanh_done, 1)
                        seed_next_gate(i, u, 1, ps_c, c_T_done, c_seeded)
                    if mid and u == 2:
                        act.wait_ge(shifted_done, i)
                        nc.scalar.activation(expd[:, :], shifted[:, :], ACT.Exp).then_inc(expd_done, 1)
                    if u % PROP == PROP - 1:
                        if rnn:
                            rnn_tanh(i, u)
                        if gru and not last_step(i, u):
                            act.wait_ge(p_T_done, props + 1)
                            nc.scalar.activation(h_prop[:, :, :], p_T[:, :, 0:B], ACT.Tanh).then_inc(p_ready, 1)
                            seed(ps_p, bias_p[:, :]).then_inc(p_seeded, 1)
                if isinstance(i, int) and i == LAG - 1:
                    act.wait_ge(loaded_gru, 16 * 8)
                    seed(ps_p, bias_p[:, :]).then_inc(p_seeded, 1)
                    for gate, psum, T_done, seeded in ((0, ps_r, r_T_done, r_seeded), (2, ps_z, z_T_done, z_seeded),
                                                       (1, ps_c, c_T_done, c_seeded)):
                        seed_gate(i + 1, 0, gate, psum, T_done, seeded)
            all_iterations(act, iteration)


def kernel(**inputs):
    import numpy as np
    import concourse.bacc as bacc
    from concourse.bass_utils import run_bass_kernel_spmd

    a = {k: np.asarray(v) for k, v in inputs.items()}

    def by_feature(w):
        rest = w.shape[1:]
        w = w.reshape(NJ, KT, QUAD, *rest)
        return np.ascontiguousarray(np.swapaxes(w, 1, 2).reshape(P, KT, *rest))

    def by_row(b):
        return np.ascontiguousarray(np.repeat(b.reshape(NJ, P), QUAD, axis=0))

    Wr, Wz, Wh = a["L3_cond_Wr"], a["L3_cond_Wz"], a["L3_cond_Wh"]
    rc = np.stack([Wr[:D].reshape(D, NJ, P), Wh[:D].reshape(D, NJ, P)], axis=2).reshape(D, NJ, 2 * P)
    x = a["x"].reshape(B, CHUNKS, STEPS, NJ, KT, QUAD).transpose(1, 3, 5, 4, 2, 0)
    x = np.ascontiguousarray(x.reshape(CHUNKS, P, KT, ROWS))
    arrays = {
        "xT": x, "condT": by_feature(a["cond_1024"].T),
        "w_rnn_x": by_feature(a["L0_cond_Wx"]), "w_rnn_h": by_feature(a["L0_cond_Wh"]), "b_rnn": by_row(a["L0_cond_b"]),
        "w_ih": by_feature(a["L2_cond_W_ih"].T), "w_hh": by_feature(a["L2_cond_W_hh"].T),
        "b_ih": by_feature(a["L2_cond_b_ih"]), "b_hh": by_feature(a["L2_cond_b_hh"]),
        "w_rc_x": by_feature(rc), "w_z_x": by_feature(Wz[:D]),
        "w_r_h": by_feature(Wr[D:]), "w_z_h": by_feature(Wz[D:]), "w_c_h": by_feature(Wh[D:]),
        "b_rcz": np.stack([by_row(a["L3_cond_" + n]) for n in ("br", "bh", "bz")], axis=1),
        "w_p": by_feature(a["L3_cond_Wp"]), "b_p": by_row(a["L3_cond_bp"]),
    }
    nc = bacc.Bacc("TRN2", target_bir_lowering=False, num_devices=1)
    args = [nc.dram_tensor(name, v.shape, mybir.dt.from_np(v.dtype), kind="ExternalInput").ap() for name, v in arrays.items()]
    args.append(nc.dram_tensor("rnn_spill", (P, P), mybir.dt.float32, kind="Internal").ap())
    args.append(nc.dram_tensor("gates_spill", (P, 3, P), mybir.dt.float32, kind="Internal").ap())
    args.append(nc.dram_tensor("y_out", (CHUNKS, P, KT, ROWS), mybir.dt.float32, kind="ExternalOutput").ap())
    cond_resid_kernel(nc, *args)
    got = run_bass_kernel_spmd(nc, [arrays], core_ids=[0]).results[0]["y_out"]
    got = got.reshape(CHUNKS, NJ, QUAD, KT, STEPS, B).transpose(5, 0, 4, 1, 3, 2)
    return np.ascontiguousarray(got.reshape(B, T, D))
```

```python
import concourse.bass as bass
from concourse import mybir
from contextlib import ExitStack

B, T, D = 2, 2048, 512
P = 128
QUAD = 32
NJ = P // QUAD
KT = D // P
STEPS = QUAD // B
ROWS = STEPS * B
CHUNKS = T // STEPS
PROP = 4
LAG = 2
GROUPS = STEPS // PROP
HALF = STEPS // 2
FRONT = 1
PARTS = 3
SPLIT_OPS = (2 * PARTS - 1) * KT


def cond_resid_kernel(nc, xT, condT, w_rnn_x, w_rnn_h, b_rnn, w_ih, w_hh, b_ih, b_hh,
                      w_rc_x, w_z_x, w_r_h, w_z_h, w_c_h, b_rcz, w_p, b_p, rnn_spill, gates_spill, out):
    fp32, bf16 = mybir.dt.float32, mybir.dt.bfloat16
    ALU = mybir.AluOpType
    ACT = mybir.ActivationFunctionType
    ctx = ExitStack()
    with ctx:
        def sb(name, *free, dtype=fp32):
            return ctx.enter_context(nc.sbuf_tensor(name, [P, *free], dtype))[:]

        def sem(name):
            return ctx.enter_context(nc.semaphore(name))

        def piece_sems(name):
            return [sem(name + "_front"), sem(name + "_others")]

        rnn_x = sb("rnn_x", KT, D)
        rnn_h = sb("rnn_h", KT, NJ, P)
        rnn_h_parts = sb("rnn_h_parts", KT, NJ, PARTS, P, dtype=bf16)
        ih = sb("ih", KT, D)
        hh = sb("hh", KT, D)
        rc_x = sb("rc_x", KT, NJ, 2 * P)
        z_x = sb("z_x", KT, D)
        r_h = sb("r_h", KT, D)
        z_h = sb("z_h", KT, NJ, P)
        z_h_parts = sb("z_h_parts", KT, NJ, PARTS, P, dtype=bf16)
        c_h = sb("c_h", KT, D)
        prop_w = sb("prop_w", KT, D)
        bias_ih = sb("bias_ih", KT)
        bias_hh = sb("bias_hh", KT)
        bias_rnn = sb("bias_rnn", P)
        bias_rcz = sb("bias_rcz", 3, P)
        bias_p = sb("bias_p", P)
        zeros = sb("zeros", QUAD)
        cond = sb("cond", KT, B)
        ones = sb("ones", QUAD)
        x_next = sb("x_next", KT, ROWS)
        x_mid = sb("x_mid", KT, ROWS)
        rnn_hist = sb("rnn_hist", KT, ROWS)
        rnn_rows = sb("rnn_rows", P)
        gates_rows = sb("gates_rows", 3, P)
        rnn_seeds = sb("rnn_seeds", STEPS, PARTS, P)
        gates_seeds = sb("gates_seeds", STEPS, 2 + PARTS, P)
        x1 = sb("x1", KT, ROWS)
        qx = sb("qx", KT, ROWS)
        qx_half = sb("qx_half", 2, ROWS)
        qx_sum = sb("qx_sum", ROWS)
        logit = sb("logit", ROWS)
        top = sb("top", STEPS)
        shifted = sb("shifted", ROWS)
        expd = sb("expd", ROWS)
        denom = sb("denom", STEPS)
        inv = sb("inv", STEPS)
        weight = sb("weight", ROWS)
        weight1 = sb("weight1", ROWS)
        x2 = sb("x2", KT, ROWS)
        mid_T = sb("mid_T", KT, ROWS)
        mid_pre = sb("mid_pre", KT, ROWS)
        mid_tanh = sb("mid_tanh", KT, ROWS)
        x3_new = sb("x3_new", KT, ROWS)
        x3 = sb("x3", KT, ROWS)
        y = sb("y", KT, ROWS)
        h_term = sb("h_term", KT, B)
        h_term_a = sb("h_term_a", KT, B)
        h_term_T = sb("h_term_T", KT, QUAD)
        l_parts = sb("l_parts", KT, PARTS, B, dtype=bf16)
        l_rest = sb("l_rest", KT, B)
        h_parts = sb("h_parts", KT, PARTS, B, dtype=bf16)
        h_rest = sb("h_rest", KT, B)
        l_T, z_T = sb("l_T", PARTS * P), sb("z_T", PARTS * P)
        l_pre, z_pre = sb("l_pre", KT, B), sb("z_pre", KT, B)
        r_tanh, z_tanh = sb("r_tanh", KT, B), sb("z_tanh", KT, B)
        h_neg_half = sb("h_neg_half", KT, B)
        rh = sb("rh", KT, B)
        h_prop = sb("h_prop", KT, B)
        scan_mul = sb("scan_mul", KT, B, 2)
        scan_add = sb("scan_add", KT, B, 2)
        gru_hist = sb("gru_hist", STEPS, KT, B, 2)

        def bank(name):
            return ctx.enter_context(nc.psum_tensor(name, [P, 512], fp32))
        ps_r, ps_z, ps_c, ps_l, ps_p, ps_logit, ps_mid, ps_proj = (
            bank(n) for n in ("ps_r", "ps_z", "ps_c", "ps_l", "ps_p", "ps_logit", "ps_mid", "ps_proj"))

        r_T, c_T, p_T = ([bank[:, P:2 * P].rearrange("p (k r) -> p k r", k=KT)[:, k, :] for bank, k in
                          ((front, slice(0, FRONT)), (others, slice(FRONT, KT)))]
                         for front, others in ((ps_p, ps_r), (ps_p, ps_c), (ps_r, ps_p)))

        loaded_rnn, loaded_ih, loaded_gru = sem("loaded_rnn"), sem("loaded_ih"), sem("loaded_gru")
        x_next_loaded, x_mid_loaded, stored = sem("x_next_loaded"), sem("x_mid_loaded"), sem("stored")
        banks_clear, banks_open, ones_set, states_set = sem("banks_clear"), sem("banks_open"), sem("ones_set"), sem("states_set")
        h_term_product, h_term_T_done = sem("h_term_product"), sem("h_term_T_done")
        h_term_a_done, h_term_ready = sem("h_term_a_done"), sem("h_term_ready")
        l_seeded, l_product, l_T_done, l_pre_done, l_tanh_done = (
            sem(n) for n in ("l_seeded", "l_product", "l_T_done", "l_pre_done", "l_tanh_done"))
        l_high_done, l_rest_done, l_ready = sem("l_high_done"), sem("l_rest_done"), sem("l_ready")
        cond_split = sem("cond_split")
        rnn_weight_parts, z_weight_parts = sem("rnn_weight_parts"), sem("z_weight_parts")
        r_seeded, r_product = sem("r_seeded"), sem("r_product")
        r_T_done, r_tanh_done = piece_sems("r_T_done"), piece_sems("r_tanh_done")
        z_seeded, z_product, z_T_done, z_pre_done, z_tanh_done = (
            sem(n) for n in ("z_seeded", "z_product", "z_T_done", "z_pre_done", "z_tanh_done"))
        h_high_done, h_rest_done, h_parts_ready = sem("h_high_done"), sem("h_rest_done"), sem("h_parts_ready")
        c_seeded, c_product = sem("c_seeded"), sem("c_product")
        c_T_done, c_tanh_done = piece_sems("c_T_done"), piece_sems("c_tanh_done")
        h_neg_half_done, z_done, kept_done = sem("h_neg_half_done"), sem("z_done"), sem("kept_done")
        rh_ready, h_ready = piece_sems("rh_ready"), piece_sems("h_ready")
        p_seeded, p_product = sem("p_seeded"), sem("p_product")
        p_T_done, p_ready = piece_sems("p_T_done"), piece_sems("p_ready")
        x1_done, qx_done, qx_half_done, qx_sum_done = (sem(n) for n in ("x1_done", "qx_done", "qx_half_done", "qx_sum_done"))
        logit_product, logit_done, top_done, shifted_done = (sem(n) for n in ("logit_product", "logit_done", "top_done", "shifted_done"))
        expd_done, denom_done, inv_done, weight_done = (sem(n) for n in ("expd_done", "denom_done", "inv_done", "weight_done"))
        weight1_done, x2_done, mid_product, mid_T_done = (sem(n) for n in ("weight1_done", "x2_done", "mid_product", "mid_T_done"))
        mid_pre_done, mid_tanh_done, x3_new_done, rc_in_product = (sem(n) for n in ("mid_pre_done", "mid_tanh_done", "x3_new_done", "rc_in_product"))
        rc_rows_done, z_in_product, z_rows_done = (sem(n) for n in ("rc_rows_done", "z_in_product", "z_rows_done"))
        rnn_in_product, rnn_rows_done = sem("rnn_in_product"), sem("rnn_rows_done")
        rnn_spilled, gates_spilled, seeds_clear = sem("rnn_spilled"), sem("gates_spilled"), sem("seeds_clear")
        rnn_fetched = [sem("rnn_fetched_0"), sem("rnn_fetched_1")]
        gates_fetched = [sem("gates_fetched_0"), sem("gates_fetched_1")]
        y_ready, x3_ready = sem("y_ready"), sem("x3_ready")

        def after(engine, semaphore, count):
            if not isinstance(count, int) or count > 0:
                engine.wait_ge(semaphore, count)

        def running(i):
            if not isinstance(i, int):
                return True, True, True, True
            return i < CHUNKS, 1 <= i <= CHUNKS, LAG <= i, i + 2 < CHUNKS

        def next_rnn(i):
            return not isinstance(i, int) or i + 1 < CHUNKS

        def next_gru(i):
            return not isinstance(i, int) or LAG <= i + 1 < CHUNKS + LAG

        def last_step(i, u):
            return isinstance(i, int) and i == CHUNKS + LAG - 1 and u == STEPS - 1

        def first_step(i, u):
            return isinstance(i, int) and i == LAG and u == 0

        def all_iterations(engine, iteration):
            for i in range(LAG + 1):
                iteration(i)
            with engine.Fori(LAG + 1, CHUNKS - 2) as i:
                iteration(i)
            for i in range(CHUNKS - 2, CHUNKS + LAG):
                iteration(i)

        PIECES = [(slice(0, FRONT), slice(0, QUAD * FRONT)), (slice(FRONT, KT), slice(QUAD * FRONT, P))]

        block = ctx.enter_context(nc.Block())

        @block.sync
        def _(sp):
            sp.dma_start(x_next[:, :, :], xT[0, :, :, :]).then_inc(x_next_loaded, 16)
            for tile, dram in ((rnn_x, w_rnn_x), (bias_rnn, b_rnn), (cond, condT), (rnn_h.rearrange("p k j n -> p k (j n)"), w_rnn_h)):
                sp.dma_start(tile, dram).then_inc(loaded_rnn, 16)
            sp.dma_start(x_mid[:, :, :], xT[0, :, :, :]).then_inc(x_mid_loaded, 16)
            for tile, dram in ((hh, w_hh), (bias_ih, b_ih), (bias_hh, b_hh), (ih, w_ih)):
                sp.dma_start(tile, dram).then_inc(loaded_ih, 16)

            def spill_rnn(chunk):
                sp.wait_ge(rnn_rows_done, chunk + 1)
                for half in range(2):
                    after(sp, rnn_fetched[half], 16 * B * chunk)
                sp.dma_start(rnn_spill, rnn_rows[:, :]).then_inc(rnn_spilled, 16)

            def fetch_rnn(chunk, half):
                steps = slice(HALF * half, HALF * (half + 1))
                sp.wait_ge(rnn_spilled, 16 * (chunk + 1))
                after(sp, l_seeded, STEPS * chunk - STEPS + HALF * (half + 1))
                for b in range(B):
                    sp.dma_start(rnn_seeds[b:P:QUAD, steps, 0, :], rnn_spill.rearrange("(j t b) n -> j t b n", j=NJ, b=B)[:, steps, b, :])\
                      .then_inc(rnn_fetched[half], 16)

            def fetch_gates(chunk, half):
                steps = slice(HALF * half, HALF * (half + 1))
                sp.wait_ge(gates_spilled, 16 * (chunk + 1))
                for seeded in (r_seeded, z_seeded, c_seeded):
                    after(sp, seeded, STEPS * chunk - STEPS + HALF * (half + 1))
                for b in range(B):
                    sp.dma_start(gates_seeds[b:P:QUAD, steps, 0:3, :],
                                 gates_spill.rearrange("(j t b) g n -> j t b g n", j=NJ, b=B)[:, steps, b, :, :])\
                      .then_inc(gates_fetched[half], 16)

            sp.wait_ge(rnn_in_product, 1)
            sp.dma_start(x_next[:, :, :], xT[1, :, :, :]).then_inc(x_next_loaded, 16)
            sp.wait_ge(seeds_clear, 3)
            spill_rnn(0)
            fetch_rnn(0, 0)
            fetch_rnn(0, 1)
            for tile, dram in ((rc_x, w_rc_x), (z_x, w_z_x), (bias_rcz, b_rcz), (bias_p, b_p), (r_h, w_r_h), (z_h.rearrange("p k j n -> p k (j n)"), w_z_h),
                               (c_h, w_c_h), (prop_w, w_p)):
                sp.dma_start(tile, dram).then_inc(loaded_gru, 16)

            def iteration(i):
                rnn, mid, gru, proj = running(i)
                if proj:
                    sp.wait_ge(rnn_in_product, i + 2)
                    sp.dma_start(x_next[:, :, :], xT[i + 2, :, :, :]).then_inc(x_next_loaded, 16)
                if mid and (not isinstance(i, int) or i < CHUNKS):
                    sp.wait_ge(x1_done, i)
                    sp.dma_start(x_mid[:, :, :], xT[i, :, :, :]).then_inc(x_mid_loaded, 16)
                if next_rnn(i):
                    spill_rnn(i + 1)
                    fetch_rnn(i + 1, 0)
                if mid:
                    sp.wait_ge(rc_rows_done, i)
                    sp.wait_ge(z_rows_done, i)
                    for half in range(2):
                        after(sp, gates_fetched[half], 16 * B * (i - 1))
                    sp.dma_start(gates_spill, gates_rows[:, :, :]).then_inc(gates_spilled, 16)
                    fetch_gates(i - 1, 0)
                    fetch_gates(i - 1, 1)
                if next_rnn(i):
                    fetch_rnn(i + 1, 1)
                if gru:
                    sp.wait_ge(y_ready, i - LAG + 1)
                    sp.dma_start(out[i - LAG, :, :, :], y[:, :, :]).then_inc(stored, 16)
            all_iterations(sp, iteration)
            sp.wait_ge(stored, 16 * CHUNKS)

        @block.gpsimd
        def _(pool):
            tt = nc.gpsimd.tensor_tensor
            nc.gpsimd.memset(ones[:, :], 1.0).then_inc(ones_set, 1)

            nc.gpsimd.memset(rnn_seeds[:, :, :, :], 0.0).then_inc(seeds_clear, 1)
            nc.gpsimd.memset(gates_seeds[:, :, :, :], 0.0).then_inc(seeds_clear, 1)
            nc.gpsimd.memset(zeros[:, :], 0.0).then_inc(seeds_clear, 1)
            pool.wait_ge(loaded_rnn, 16 * 4)
            pool.wait_ge(loaded_ih, 16 * 4)
            pool.wait_ge(h_term_T_done, 1)
            tt(h_term_a[:, :, :], h_term_T[:, :, 0:B], bias_hh[:, :].unsqueeze(2).to_broadcast([P, KT, B]), ALU.add).then_inc(h_term_a_done, 1)
            pool.wait_ge(h_term_a_done, 1)
            tt(h_term[:, :, :], h_term_a[:, :, :], bias_ih[:, :].unsqueeze(2).to_broadcast([P, KT, B]), ALU.add).then_inc(h_term_ready, 1)
            pool.wait_ge(h_term_ready, 1)

            def iteration(i):
                rnn, mid, gru, proj = running(i)
                if mid:
                    pool.wait_ge(l_tanh_done, STEPS * i)
                    pool.wait_ge(x_mid_loaded, 16 * i)
                    tt(x1[:, :, :], x_mid[:, :, :], rnn_hist[:, :, :], ALU.add).then_inc(x1_done, 1)
                    pool.wait_ge(x1_done, i)
                    for k in range(KT):
                        last = tt(qx[:, k, :].rearrange("p (t b) -> p t b", b=B), x1[:, k, :].rearrange("p (t b) -> p t b", b=B),
                                  cond[:, k, :].unsqueeze(1).to_broadcast([P, STEPS, B]), ALU.mult)
                    last.then_inc(qx_done, 1)
                    pool.wait_ge(qx_done, i)
                    tt(qx_half[:, :, :], qx[:, 0:2, :], qx[:, 2:4, :], ALU.add).then_inc(qx_half_done, 1)
                    pool.wait_ge(qx_half_done, i)
                    tt(qx_sum[:, :], qx_half[:, 0, :], qx_half[:, 1, :], ALU.add).then_inc(qx_sum_done, 1)
                    pool.wait_ge(top_done, i)
                    pair = logit[:, :].rearrange("p (t b) -> p t b", b=B)
                    tt(shifted[:, :].rearrange("p (t b) -> p t b", b=B), pair, top[:, :].unsqueeze(2).to_broadcast([P, STEPS, B]),
                       ALU.subtract).then_inc(shifted_done, 1)
                    pool.wait_ge(expd_done, i)
                    epair = expd[:, :].rearrange("p (t b) -> p t b", b=B)
                    tt(denom[:, :], epair[:, :, 0], epair[:, :, 1], ALU.add).then_inc(denom_done, 1)
                    pool.wait_ge(inv_done, i)
                    tt(weight[:, :].rearrange("p (t b) -> p t b", b=B), epair, inv[:, :].unsqueeze(2).to_broadcast([P, STEPS, B]),
                       ALU.mult).then_inc(weight_done, 1)
                    pool.wait_ge(weight_done, i)
                    tt(weight1[:, :], weight[:, :], ones[:, :], ALU.add).then_inc(weight1_done, 1)
                    pool.wait_ge(weight1_done, i)
                    tt(x2[:, :, :], x1[:, :, :], weight1[:, :].unsqueeze(1).to_broadcast([P, KT, ROWS]), ALU.mult).then_inc(x2_done, 1)
                    pool.wait_ge(mid_T_done, i)
                    for k in range(KT):
                        last = tt(mid_pre[:, k, :].rearrange("p (t b) -> p t b", b=B), mid_T[:, k, :].rearrange("p (t b) -> p t b", b=B),
                                  h_term[:, k, :].unsqueeze(1).to_broadcast([P, STEPS, B]), ALU.add)
                    last.then_inc(mid_pre_done, 1)
                    pool.wait_ge(mid_tanh_done, i)
                    tt(x3_new[:, :, :], x2[:, :, :], mid_tanh[:, :, :], ALU.add).then_inc(x3_new_done, 1)
                if gru:
                    pool.wait_ge(h_ready[1], STEPS * (i - LAG + 1))
                    after(pool, stored, 16 * (i - LAG))
                    for k in range(KT):
                        last = tt(y[:, k, :].rearrange("p (t b) -> p t b", b=B), x3[:, k, :].rearrange("p (t b) -> p t b", b=B),
                                  gru_hist[:, :, k, :, 1], ALU.add)
                    last.then_inc(y_ready, 1)
                    pool.wait_ge(y_ready, i - LAG + 1)
                if mid:
                    tt(x3[:, :, :], x2[:, :, :], mid_tanh[:, :, :], ALU.add).then_inc(x3_ready, 1)
                    pool.wait_ge(x3_ready, i)
            all_iterations(pool, iteration)

        @block.tensor
        def _(pe):
            def product(psum, rows, stationary, weights, width=P, tiles=range(KT)):
                for k in tiles:
                    for j in range(NJ):
                        last = nc.tensor.matmul(psum[QUAD * j:QUAD * j + rows, 0:width], stationary(k), weights(k, j),
                                                start=(k == 0), stop=(k == KT - 1))
                return last

            def seeded_product(psum, stationary, w, ready, count):
                for k in range(KT):
                    if ready is not None and k in (0, FRONT):
                        pe.wait_ge(ready[k // FRONT], count)
                    for j in range(NJ):
                        last = nc.tensor.matmul(psum[QUAD * j:QUAD * j + B, 0:P], stationary(k), w[:, k, P * j:P * (j + 1)],
                                                start=False, stop=(k == KT - 1), skip_group_check=True)
                return last

            def product_in_parts(psum, state_parts, w_parts):
                for k in range(KT):
                    for j in range(NJ):
                        last = nc.tensor.matmul(psum[QUAD * j:QUAD * j + PARTS * B, 0:PARTS * P],
                                                state_parts[:, k, :, :].rearrange("p q b -> p (q b)"),
                                                w_parts[:, k, j, :, :].rearrange("p q n -> p (q n)"),
                                                start=False, stop=(k == KT - 1), skip_group_check=True)
                return last

            def open_bank(psum, width=P):
                for j in range(NJ):
                    last = nc.tensor.matmul(psum[QUAD * j:QUAD * (j + 1), 0:width], zeros[:, :], rnn_x[:, 0, 0:width], start=True, stop=True)
                return last

            def columns(w):
                return lambda k, j: w[:, k, P * j:P * (j + 1)]

            def project_rnn_input(chunk, tiles=range(KT)):
                if tiles[0] == 0:
                    pe.wait_ge(x_next_loaded, 16 * (chunk + 1))
                    after(pe, rnn_rows_done, chunk)
                last = product(ps_proj, ROWS, lambda k: x_next[:, k, :], columns(rnn_x), tiles=tiles)
                if tiles[-1] == KT - 1:
                    last.then_inc(rnn_in_product, 1)

            pe.wait_ge(banks_clear, 1)
            pe.wait_ge(loaded_rnn, 16 * 4)
            project_rnn_input(0)
            pe.wait_ge(seeds_clear, 3)
            for psum in (ps_l, ps_z):
                open_bank(psum, PARTS * P).then_inc(banks_open, 1)
            for psum in (ps_p, ps_r, ps_c):
                open_bank(psum).then_inc(banks_open, 1)
            project_rnn_input(1)
            pe.wait_ge(loaded_ih, 16 * 4)
            product(ps_mid, B, lambda k: cond[:, k, :], columns(hh)).then_inc(h_term_product, 1)
            pe.wait_ge(states_set, 2)
            pe.wait_ge(rnn_weight_parts, SPLIT_OPS)
            pe.wait_ge(ones_set, 1)

            MID = {3: (0, 1, 2), 4: (3,)}
            RC_IN = {7: (0, 1), 11: (2, 3)}
            Z_IN = {8: (0,), 9: (1,), 10: (2,), 12: (3,)}
            RNN_IN = {14: (0,), 15: (1, 2, 3)}

            def iteration(i):
                rnn, mid, gru, proj = running(i)
                if isinstance(i, int) and i == 1:
                    pe.wait_ge(loaded_gru, 16 * 8)
                if isinstance(i, int) and i == LAG:
                    pe.wait_ge(z_weight_parts, SPLIT_OPS)
                for u in range(STEPS):
                    t_rnn = STEPS * i + u
                    t_gru = STEPS * (i - LAG) + u
                    props = GROUPS * (i - LAG) + u // PROP
                    if gru:
                        if u % PROP == 0:
                            ready, count = (p_ready, props) if not first_step(i, u) else (None, None)
                            state = lambda k: h_prop[:, k, :]
                        else:
                            ready, count = h_ready, t_gru
                            state = lambda k: gru_hist[:, u - 1, k, :, 1]
                        pe.wait_ge(r_seeded, t_gru + 1)
                        seeded_product(ps_r, state, r_h, ready, count).then_inc(r_product, 1)
                        pe.wait_ge(z_seeded, t_gru + 1)
                        pe.wait_ge(h_parts_ready, t_gru + 1)
                        product_in_parts(ps_z, h_parts, z_h_parts).then_inc(z_product, 1)
                        pe.wait_ge(c_seeded, t_gru + 1)
                        seeded_product(ps_c, lambda k: rh[:, k, :], c_h, rh_ready, t_gru + 1).then_inc(c_product, 1)
                    if rnn:
                        after(pe, l_ready, t_rnn)
                        pe.wait_ge(l_seeded, t_rnn + 1)
                        product_in_parts(ps_l, l_parts, rnn_h_parts).then_inc(l_product, 1)
                    if mid and u == 1:
                        pe.wait_ge(qx_sum_done, i)
                        for j in range(NJ):
                            last = nc.tensor.matmul(ps_logit[QUAD * j:QUAD * (j + 1), 0:ROWS], ones[:, :], qx_sum[:, :], start=True, stop=True)
                        last.then_inc(logit_product, 1)
                    if u % PROP == PROP - 1:
                        if gru and not last_step(i, u):
                            pe.wait_ge(p_seeded, props + 1)
                            seeded_product(ps_p, lambda k: gru_hist[:, u, k, :, 1], prop_w, h_ready, t_gru + 1).then_inc(p_product, 1)
                    if mid and u in MID:
                        if 0 in MID[u]:
                            pe.wait_ge(x2_done, i)
                        last = product(ps_mid, ROWS, lambda k: x2[:, k, :], columns(ih), tiles=MID[u])
                        if KT - 1 in MID[u]:
                            last.then_inc(mid_product, 1)
                    if mid and u in RC_IN:
                        if 0 in RC_IN[u]:
                            pe.wait_ge(x3_new_done, i)
                        last = product(ps_mid, ROWS, lambda k: x3_new[:, k, :], lambda k, j: rc_x[:, k, j, :], 2 * P, RC_IN[u])
                        if KT - 1 in RC_IN[u]:
                            last.then_inc(rc_in_product, 1)
                    if mid and u in Z_IN:
                        if 0 in Z_IN[u]:
                            pe.wait_ge(rnn_rows_done, i + 2 if not isinstance(i, int) else min(i + 2, CHUNKS))
                        last = product(ps_proj, ROWS, lambda k: x3_new[:, k, :], columns(z_x), tiles=Z_IN[u])
                        if KT - 1 in Z_IN[u]:
                            last.then_inc(z_in_product, 1)
                    if proj and u in RNN_IN:
                        if 0 in RNN_IN[u] and mid:
                            pe.wait_ge(z_rows_done, i)
                        project_rnn_input(i + 2, RNN_IN[u])
            all_iterations(pe, iteration)

        @block.vector
        def _(dve):
            tt = nc.vector.tensor_tensor
            for psum in (ps_r, ps_z, ps_c, ps_l, ps_p, ps_logit, ps_mid, ps_proj):
                last = nc.vector.memset(psum[:, :], 0.0)
            last.then_inc(banks_clear, 1)
            nc.vector.memset(scan_mul[:, :, :, :], 0.0).then_inc(banks_clear, 1)
            dve.wait_ge(banks_clear, 2)

            def transposed(tile, psum):
                return nc.vector.transpose(tile, psum[:, 0:P])

            def transpose_piece(n, pieces, psum, T_done):
                nc.vector.transpose(pieces[n].rearrange("p k r -> p (k r)"), psum[:, PIECES[n][1]]).then_inc(T_done[n], 1)

            def pieces_transposed(pieces, psum, T_done):
                for n in range(2):
                    transpose_piece(n, pieces, psum, T_done)

            def flat(tile):
                return tile.rearrange("p k r -> p (k r)")

            def rnn_input_rows(chunk):
                dve.wait_ge(rnn_in_product, chunk + 1)
                after(dve, rnn_spilled, 16 * chunk)
                tt(rnn_rows[:, :], ps_proj[:, 0:P], bias_rnn[:, :], ALU.add).then_inc(rnn_rows_done, 1)

            dve.wait_ge(loaded_rnn, 16 * 4)
            rnn_input_rows(0)
            nc.vector.tensor_copy(h_prop[:, :, :], cond[:, :, :]).then_inc(states_set, 1)
            nc.vector.tensor_copy(l_parts[:, :, 0, :], cond[:, :, :]).then_inc(cond_split, 1)
            dve.wait_ge(cond_split, 1)
            tt(l_rest[:, :, :], cond[:, :, :], l_parts[:, :, 0, :], ALU.subtract)
            tt(l_parts[:, :, 1, :], cond[:, :, :], l_parts[:, :, 0, :], ALU.subtract).then_inc(cond_split, 1)
            dve.wait_ge(cond_split, 2)
            tt(l_parts[:, :, 2, :], l_rest[:, :, :], l_parts[:, :, 1, :], ALU.subtract).then_inc(states_set, 1)

            def split_weights(w, w_parts, done, ops):
                for n in ops:
                    stage, k = n // KT, n % KT
                    after(dve, done, n - KT + 1)
                    if stage % 2 == 0:
                        nc.vector.tensor_copy(w_parts[:, k, :, stage // 2, :], w[:, k, :, :]).then_inc(done, 1)
                    else:
                        tt(w[:, k, :, :], w[:, k, :, :], w_parts[:, k, :, stage // 2, :], ALU.subtract).then_inc(done, 1)
            split_weights(rnn_h, rnn_h_parts, rnn_weight_parts, range(SPLIT_OPS))
            dve.wait_ge(h_term_product, 1)
            transposed(flat(h_term_T[:, :, :]), ps_mid).then_inc(h_term_T_done, 1)
            rnn_input_rows(1)
            dve.wait_ge(states_set, 2)

            def summed(pre, tile):
                return nc.vector.tensor_reduce(pre[:, :, :], tile.rearrange("p (w k r) -> p k r w", w=PARTS, k=KT)[:, :, 0:PARTS * B, :]
                                               .rearrange("p k (q b) w -> p k b w q", b=B), mybir.AxisListType.XY, ALU.add)

            def rnn_T(i, u):
                dve.wait_ge(l_product, STEPS * i + u + 1)
                nc.vector.transpose(l_T[:, :], ps_l[:, 0:PARTS * P]).then_inc(l_T_done, 1)

            def rnn_pre(i, u):
                dve.wait_ge(l_T_done, STEPS * i + u + 1)
                summed(l_pre, l_T).then_inc(l_pre_done, 1)

            def rnn_rest(i, u):
                t = STEPS * i + u
                dve.wait_ge(l_tanh_done, t + 1)
                dve.wait_ge(l_high_done, t + 1)
                for tile in (l_rest[:, :, :], l_parts[:, :, 1, :]):
                    last = tt(tile, rnn_hist[:, :, B * u:B * (u + 1)], l_parts[:, :, 0, :], ALU.subtract)
                last.then_inc(l_rest_done, 1)

            def rnn_low(i, u):
                dve.wait_ge(l_rest_done, STEPS * i + u + 1)
                tt(l_parts[:, :, 2, :], l_rest[:, :, :], l_parts[:, :, 1, :], ALU.subtract).then_inc(l_ready, 1)

            def gru_high_middle(i, u):
                t = STEPS * (i - LAG) + u
                if u % PROP == 0:
                    after(dve, p_ready[1], GROUPS * (i - LAG) + u // PROP)
                    state = h_prop[:, :, :]
                else:
                    dve.wait_ge(h_ready[1], t)
                    state = gru_hist[:, u - 1, :, :, 1]
                after(dve, z_product, t)
                nc.vector.tensor_copy(h_parts[:, :, 0, :], state).then_inc(h_high_done, 1)
                nc.vector.tensor_scalar(h_neg_half[:, :, :], state, -0.5, None, ALU.mult).then_inc(h_neg_half_done, 1)
                dve.wait_ge(h_high_done, t + 1)
                tt(h_rest[:, :, :], state, h_parts[:, :, 0, :], ALU.subtract)
                tt(h_parts[:, :, 1, :], state, h_parts[:, :, 0, :], ALU.subtract).then_inc(h_rest_done, 1)

            def gru_low(i, u):
                dve.wait_ge(h_rest_done, STEPS * (i - LAG) + u + 1)
                tt(h_parts[:, :, 2, :], h_rest[:, :, :], h_parts[:, :, 1, :], ALU.subtract).then_inc(h_parts_ready, 1)

            def iteration(i):
                rnn, mid, gru, proj = running(i)
                for u in range(STEPS):
                    t = STEPS * (i - LAG) + u
                    props = GROUPS * (i - LAG) + u // PROP
                    if gru and u > 0:
                        gru_high_middle(i, u)
                    if rnn and u % PROP:
                        rnn_T(i, u - 1)
                    if gru and u > 0:
                        gru_low(i, u)
                    if rnn and u % PROP:
                        rnn_pre(i, u - 1)
                        if not gru:
                            rnn_rest(i, u - 1)
                            rnn_low(i, u - 1)
                    if gru:
                        if u % PROP == 0:
                            dve.wait_ge(p_seeded, props + 1)
                        dve.wait_ge(r_product, t + 1)
                        pieces_transposed(r_T, ps_r, r_T_done)
                        for n, (k, _) in enumerate(PIECES):
                            dve.wait_ge(r_tanh_done[n], t + 1)
                            if n == 0:
                                dve.wait_ge(h_neg_half_done, t + 1)
                            nc.vector.scalar_tensor_tensor(rh[:, k, :], r_tanh[:, k, :], 1.0, h_neg_half[:, k, :], ALU.subtract, ALU.mult).then_inc(rh_ready[n], 1)
                        if rnn and u % PROP:
                            rnn_rest(i, u - 1)
                        dve.wait_ge(z_product, t + 1)
                        nc.vector.transpose(z_T[:, :], ps_z[:, 0:PARTS * P]).then_inc(z_T_done, 1)
                        if rnn and u % PROP:
                            rnn_low(i, u - 1)
                        dve.wait_ge(z_T_done, t + 1)
                        summed(z_pre, z_T).then_inc(z_pre_done, 1)
                    if u == 0 and mid and next_rnn(i):
                        rnn_input_rows(i + 1)
                    if mid and u == 5:
                        dve.wait_ge(mid_product, i)
                        transposed(flat(mid_T[:, :, :]), ps_mid).then_inc(mid_T_done, 1)
                    if mid and u == 12:
                        dve.wait_ge(rc_in_product, i)
                        if isinstance(i, int) and i == 1:
                            dve.wait_ge(loaded_gru, 16 * 8)
                        after(dve, gates_spilled, 16 * (i - 1))
                        tt(gates_rows[:, 0:2, :].rearrange("p g n -> p (g n)"), ps_mid[:, 0:2 * P],
                           bias_rcz[:, 0:2, :].rearrange("p g n -> p (g n)"), ALU.add).then_inc(rc_rows_done, 1)
                    if mid and u == 13:
                        dve.wait_ge(z_in_product, i)
                        tt(gates_rows[:, 2, :], ps_proj[:, 0:P], bias_rcz[:, 2, :], ALU.add).then_inc(z_rows_done, 1)
                    if mid and u == 2:
                        dve.wait_ge(logit_product, i)
                        nc.vector.tensor_scalar(logit[:, :], ps_logit[:, 0:ROWS], float(D) ** -0.5, None, ALU.mult).then_inc(logit_done, 1)
                        dve.wait_ge(logit_done, i)
                        pair = logit[:, :].rearrange("p (t b) -> p t b", b=B)
                        tt(top[:, :], pair[:, :, 0], pair[:, :, 1], ALU.max).then_inc(top_done, 1)
                    if mid and u == 3:
                        dve.wait_ge(denom_done, i)
                        nc.vector.reciprocal(inv[:, :], denom[:, :]).then_inc(inv_done, 1)
                    if gru:
                        dve.wait_ge(c_product, t + 1)
                        transpose_piece(0, c_T, ps_c, c_T_done)
                        dve.wait_ge(z_tanh_done, t + 1)
                        nc.vector.scalar_tensor_tensor(scan_add[:, :, :, 1], z_tanh[:, :, :], 1.0, h_neg_half[:, :, :], ALU.subtract, ALU.mult).then_inc(kept_done, 1)
                        transpose_piece(1, c_T, ps_c, c_T_done)
                        dve.wait_ge(z_done, t + 1)
                        dve.wait_ge(kept_done, t + 1)
                        if u == 0:
                            after(dve, y_ready, i - LAG)
                        for n, (k, _) in enumerate(PIECES):
                            dve.wait_ge(c_tanh_done[n], t + 1)
                            nc.vector.tensor_tensor_scan(gru_hist[:, u, k, :, :].rearrange("p k b s -> p (k b s)"),
                                                         scan_mul[:, k, :, :].rearrange("p k b s -> p (k b s)"),
                                                         scan_add[:, k, :, :].rearrange("p k b s -> p (k b s)"),
                                                         0.0, ALU.mult, ALU.add).then_inc(h_ready[n], 1)
                    if u % PROP == PROP - 1:
                        if rnn:
                            rnn_T(i, u)
                            rnn_pre(i, u)
                        if gru and not last_step(i, u):
                            dve.wait_ge(p_product, props + 1)
                            pieces_transposed(p_T, ps_p, p_T_done)
                        if rnn:
                            rnn_rest(i, u)
                            rnn_low(i, u)
                    if isinstance(i, int) and i == LAG - 1:
                        if u == 0:
                            dve.wait_ge(loaded_gru, 16 * 8)
                        split_weights(z_h, z_h_parts, z_weight_parts, range(SPLIT_OPS * u // STEPS, SPLIT_OPS * (u + 1) // STEPS))
                if next_gru(i):
                    gru_high_middle(i + 1, 0)
                    gru_low(i + 1, 0)
            all_iterations(dve, iteration)

        @block.scalar
        def _(act):
            def seed(psum, rows, width=P):
                return nc.scalar.activation(psum[:, 0:width], rows, ACT.Copy)

            def seed_rnn(i, u):
                if u % HALF == 0:
                    act.wait_ge(rnn_fetched[u // HALF], 16 * B * (i + 1))
                after(act, l_T_done, STEPS * i + u)
                seed(ps_l, rnn_seeds[:, u, :, :].rearrange("p q n -> p (q n)"), PARTS * P).then_inc(l_seeded, 1)

            def seed_gate(i, u, gate, psum, T_done, seeded):
                if u % HALF == 0:
                    act.wait_ge(gates_fetched[u // HALF], 16 * B * (i - LAG + 1))
                after(act, T_done, STEPS * (i - LAG) + u)
                if gate == 2:
                    seed(psum, gates_seeds[:, u, 2:, :].rearrange("p q n -> p (q n)"), PARTS * P).then_inc(seeded, 1)
                else:
                    seed(psum, gates_seeds[:, u, gate, :]).then_inc(seeded, 1)

            def seed_next_gate(i, u, gate, psum, T_done, seeded):
                if u < STEPS - 1:
                    seed_gate(i, u + 1, gate, psum, T_done, seeded)
                elif next_gru(i):
                    seed_gate(i + 1, 0, gate, psum, T_done, seeded)

            def rnn_tanh(i, u):
                act.wait_ge(l_pre_done, STEPS * i + u + 1)
                if u == 0 and not (isinstance(i, int) and i == 0):
                    act.wait_ge(x1_done, i)
                nc.scalar.activation(rnn_hist[:, :, B * u:B * (u + 1)], l_pre[:, :, :], ACT.Tanh).then_inc(l_tanh_done, 1)

            def rnn_high(i, u):
                act.wait_ge(l_pre_done, STEPS * i + u + 1)
                nc.scalar.activation(l_parts[:, :, 0, :], l_pre[:, :, :], ACT.Tanh).then_inc(l_high_done, 1)

            act.wait_ge(banks_open, 5)
            act.wait_ge(states_set, 2)

            def iteration(i):
                rnn, mid, gru, proj = running(i)
                for u in range(STEPS):
                    t = STEPS * (i - LAG) + u
                    props = GROUPS * (i - LAG) + u // PROP
                    if rnn and u % PROP:
                        rnn_tanh(i, u - 1)
                    if mid and u == 6:
                        act.wait_ge(mid_pre_done, i)
                        nc.scalar.activation(mid_tanh[:, :, :], mid_pre[:, :, :], ACT.Tanh).then_inc(mid_tanh_done, 1)
                    if gru:
                        for n, (k, _) in enumerate(PIECES):
                            act.wait_ge(r_T_done[n], t + 1)
                            nc.scalar.activation(r_tanh[:, k, :], r_T[n][:, :, 0:B], ACT.Tanh, scale=-0.5).then_inc(r_tanh_done[n], 1)
                    if rnn and u % PROP:
                        rnn_high(i, u - 1)
                    if rnn:
                        seed_rnn(i, u)
                    if gru:
                        seed_next_gate(i, u, 0, ps_r, r_T_done[1], r_seeded)
                        act.wait_ge(z_pre_done, t + 1)
                        nc.scalar.activation(z_tanh[:, :, :], z_pre[:, :, :], ACT.Tanh, scale=0.5).then_inc(z_tanh_done, 1)
                        act.wait_ge(z_tanh_done, t + 1)
                        nc.scalar.activation(scan_mul[:, :, :, 1], z_tanh[:, :, :], ACT.Copy, bias=0.5, scale=0.5).then_inc(z_done, 1)
                        for n, (k, _) in enumerate(PIECES):
                            act.wait_ge(c_T_done[n], t + 1)
                            nc.scalar.activation(scan_add[:, k, :, 0], c_T[n][:, :, 0:B], ACT.Tanh).then_inc(c_tanh_done[n], 1)
                        seed_next_gate(i, u, 1, ps_c, c_T_done[1], c_seeded)
                        seed_next_gate(i, u, 2, ps_z, z_T_done, z_seeded)
                    if mid and u == 2:
                        act.wait_ge(shifted_done, i)
                        nc.scalar.activation(expd[:, :], shifted[:, :], ACT.Exp).then_inc(expd_done, 1)
                    if u % PROP == PROP - 1:
                        if rnn:
                            rnn_tanh(i, u)
                            rnn_high(i, u)
                        if gru and not last_step(i, u):
                            for n, (k, _) in enumerate(PIECES):
                                act.wait_ge(p_T_done[n], props + 1)
                                nc.scalar.activation(h_prop[:, k, :], p_T[n][:, :, 0:B], ACT.Tanh).then_inc(p_ready[n], 1)
                            seed(ps_p, bias_p[:, :]).then_inc(p_seeded, 1)
                if isinstance(i, int) and i == LAG - 1:
                    act.wait_ge(loaded_gru, 16 * 8)
                    seed(ps_p, bias_p[:, :]).then_inc(p_seeded, 1)
                    for gate, psum, T_done, seeded in ((0, ps_r, r_T_done[1], r_seeded), (2, ps_z, z_T_done, z_seeded),
                                                       (1, ps_c, c_T_done[1], c_seeded)):
                        seed_gate(i + 1, 0, gate, psum, T_done, seeded)
            all_iterations(act, iteration)


def kernel(**inputs):
    import numpy as np
    import concourse.bacc as bacc
    from concourse.bass_utils import run_bass_kernel_spmd

    a = {k: np.asarray(v) for k, v in inputs.items()}

    def by_feature(w):
        rest = w.shape[1:]
        w = w.reshape(NJ, KT, QUAD, *rest)
        return np.ascontiguousarray(np.swapaxes(w, 1, 2).reshape(P, KT, *rest))

    def by_row(b):
        return np.ascontiguousarray(np.repeat(b.reshape(NJ, P), QUAD, axis=0))

    Wr, Wz, Wh = a["L3_cond_Wr"], a["L3_cond_Wz"], a["L3_cond_Wh"]
    rc = np.stack([Wr[:D].reshape(D, NJ, P), Wh[:D].reshape(D, NJ, P)], axis=2).reshape(D, NJ, 2 * P)
    x = a["x"].reshape(B, CHUNKS, STEPS, NJ, KT, QUAD).transpose(1, 3, 5, 4, 2, 0)
    x = np.ascontiguousarray(x.reshape(CHUNKS, P, KT, ROWS))
    arrays = {
        "xT": x, "condT": by_feature(a["cond_1024"].T),
        "w_rnn_x": by_feature(a["L0_cond_Wx"]), "w_rnn_h": by_feature(a["L0_cond_Wh"]), "b_rnn": by_row(a["L0_cond_b"]),
        "w_ih": by_feature(a["L2_cond_W_ih"].T), "w_hh": by_feature(a["L2_cond_W_hh"].T),
        "b_ih": by_feature(a["L2_cond_b_ih"]), "b_hh": by_feature(a["L2_cond_b_hh"]),
        "w_rc_x": by_feature(rc), "w_z_x": by_feature(Wz[:D]),
        "w_r_h": by_feature(Wr[D:]), "w_z_h": by_feature(Wz[D:]), "w_c_h": by_feature(Wh[D:]),
        "b_rcz": np.stack([by_row(a["L3_cond_" + n]) for n in ("br", "bh", "bz")], axis=1),
        "w_p": by_feature(a["L3_cond_Wp"]), "b_p": by_row(a["L3_cond_bp"]),
    }
    nc = bacc.Bacc("TRN2", target_bir_lowering=False, num_devices=1)
    args = [nc.dram_tensor(name, v.shape, mybir.dt.from_np(v.dtype), kind="ExternalInput").ap() for name, v in arrays.items()]
    args.append(nc.dram_tensor("rnn_spill", (P, P), mybir.dt.float32, kind="Internal").ap())
    args.append(nc.dram_tensor("gates_spill", (P, 3, P), mybir.dt.float32, kind="Internal").ap())
    args.append(nc.dram_tensor("y_out", (CHUNKS, P, KT, ROWS), mybir.dt.float32, kind="ExternalOutput").ap())
    cond_resid_kernel(nc, *args)
    got = run_bass_kernel_spmd(nc, [arrays], core_ids=[0]).results[0]["y_out"]
    got = got.reshape(CHUNKS, NJ, QUAD, KT, STEPS, B).transpose(5, 0, 4, 1, 3, 2)
    return np.ascontiguousarray(got.reshape(B, T, D))
```
